# Optimizing a Trainium2 kernel written in Bass

```python
import numpy as np
import jax
import jax.numpy as jnp

def _softmax(x, axis=-1):
    return jax.nn.softmax(x, axis=axis)

def _gelu(x):
    return jax.nn.gelu(x, approximate=True)

def _silu(x):
    return jax.nn.silu(x)

def _sigmoid(x):
    return jax.nn.sigmoid(x)

def _layernorm(x, axis=-1, eps=1e-05):
    m = jnp.mean(x, axis=axis, keepdims=True)
    v = jnp.var(x, axis=axis, keepdims=True)
    return (x - m) / jnp.sqrt(v + eps)

def _scatter_add(tgt, idx, src, axis=0):
    return tgt.at[idx].add(src)

def _segment_sum(src, seg, n):
    return jax.ops.segment_sum(src, seg, n)
kernel_name = 'mk_recurrent_d2_jaxref_r8_6f2ba1'

def setup_inputs(seed: int=0):
    np.random.seed(seed)
    _w = jnp.asarray

    def _L0_attn_setup():
        import jax, jax.numpy as jnp
        import numpy as np
        B, S, HID = (2, 256, 256)
        H, HKV, D = (16, 4, 128)
        ROPE_BASE = 1000000.0
        EPS = 1e-05

        def _layernorm(x, g, b):
            mu = jnp.mean(x, axis=-1, keepdims=True)
            var = jnp.mean(jnp.square(x - mu), axis=-1, keepdims=True)
            return (x - mu) * jax.lax.rsqrt(var + EPS) * g + b

        def _rope_tables(seq_len, dim, base):
            inv_freq = 1.0 / base ** (jnp.arange(0, dim, 2, dtype=jnp.float32) / dim)
            t = jnp.arange(seq_len, dtype=jnp.float32)
            freqs = jnp.outer(t, inv_freq)
            cos = jnp.concatenate([jnp.cos(freqs), jnp.cos(freqs)], axis=-1)
            sin = jnp.concatenate([jnp.sin(freqs), jnp.sin(freqs)], axis=-1)
            return (cos, sin)

        def _rotate_half(x):
            x1, x2 = jnp.split(x, 2, axis=-1)
            return jnp.concatenate([-x2, x1], axis=-1)
        key = jax.random.key(seed)
        k1, k2, k3 = jax.random.split(key, 3)
        return {'x': jax.random.normal(k1, (B, S, HID), dtype=jnp.float32), 'w_qkv': jax.random.normal(k2, ((H + 2 * HKV) * D, HID), dtype=jnp.float32) * 0.02, 'w_o': jax.random.normal(k3, (HID, H * D), dtype=jnp.float32) * 0.02, 'qn_g': jnp.ones((D,), jnp.float32), 'qn_b': jnp.zeros((D,), jnp.float32), 'kn_g': jnp.ones((D,), jnp.float32), 'kn_b': jnp.zeros((D,), jnp.float32)}
    _L0_attn_in = _L0_attn_setup()

    def _L0_ffn_setup():
        import jax, jax.numpy as jnp
        import numpy as np
        import math
        B, S, D = (2, 128, 256)
        H, KVH, HD = (16, 4, 128)
        E, K, FF = (8, 2, 896)
        EPS = 1e-05
        ROPE_BASE = 1000000.0

        def rmsnorm(x, w, eps=EPS):
            xf = x.astype(jnp.float32)
            var = jnp.mean(xf * xf, axis=-1, keepdims=True)
            return (xf * jax.lax.rsqrt(var + eps)).astype(x.dtype) * w

        def apply_rope(x, cos, sin):
            x1 = x[..., 0::2]
            x2 = x[..., 1::2]
            r1 = x1 * cos - x2 * sin
            r2 = x1 * sin + x2 * cos
            return jnp.stack([r1, r2], axis=-1).reshape(x.shape)
        key = jax.random.key(seed)
        ks = jax.random.split(key, 12)
        sc = 0.02
        inp = {'x': jax.random.normal(ks[0], (B, S, D), jnp.float32), 'ln_w': jnp.ones((D,), jnp.float32), 'ff_ln_w': jnp.ones((D,), jnp.float32), 'wq': jax.random.normal(ks[1], (D, H * HD), jnp.float32) * sc, 'wk': jax.random.normal(ks[2], (D, KVH * HD), jnp.float32) * sc, 'wv': jax.random.normal(ks[3], (D, KVH * HD), jnp.float32) * sc, 'wo': jax.random.normal(ks[4], (H * HD, D), jnp.float32) * sc, 'gate_w': jax.random.normal(ks[5], (D, E), jnp.float32) * sc, 'w1': jax.random.normal(ks[6], (E, D, FF), jnp.float32) * sc, 'w3': jax.random.normal(ks[7], (E, D, FF), jnp.float32) * sc, 'w2': jax.random.normal(ks[8], (E, FF, D), jnp.float32) * sc}
        return inp
    _L0_ffn_in = _L0_ffn_setup()

    def _L1_attn_setup():
        import jax, jax.numpy as jnp
        import numpy as np
        DIM = 256
        N_HEAD = 16
        N_KV_HEAD = 4
        DQK = 128
        DV = DIM // N_HEAD
        N_REP = N_HEAD // N_KV_HEAD
        WIN = 64
        FRONT = 32
        SEQ = 512
        THETA = 10000.0

        def rope_cos_sin(seq_len, dim, theta=THETA):
            inv_freq = 1.0 / theta ** (np.arange(0, dim, 2)[:dim // 2].astype(np.float32) / dim)
            t = np.arange(seq_len, dtype=np.float32)
            ang = np.outer(t, inv_freq)
            return (jnp.asarray(np.cos(ang)), jnp.asarray(np.sin(ang)))

        def apply_rope(x, cos, sin):
            xr = x[..., 0::2]
            xi = x[..., 1::2]
            c = cos[None, :, None, :]
            s = sin[None, :, None, :]
            out_r = xr * c - xi * s
            out_i = xr * s + xi * c
            return jnp.stack([out_r, out_i], axis=-1).reshape(x.shape)

        def build_mask(seq_len, window, front):
            i = jnp.arange(seq_len)[:, None]
            j = jnp.arange(seq_len)[None, :]
            band = (j <= i) & (j > i - window)
            front_ok = (j < front) & (j <= i - window)
            allowed = band | front_ok
            return jnp.where(allowed, 0.0, -jnp.inf).astype(jnp.float32)
        key = jax.random.key(seed)
        ks = jax.random.split(key, 5)
        B = 1
        scale_in = 1.0 / np.sqrt(DIM)
        x = jax.random.normal(ks[0], (B, SEQ, DIM), dtype=jnp.float32)
        wq = jax.random.normal(ks[1], (DIM, N_HEAD * DQK), dtype=jnp.float32) * scale_in
        wk = jax.random.normal(ks[2], (DIM, N_KV_HEAD * DQK), dtype=jnp.float32) * scale_in
        wv = jax.random.normal(ks[3], (DIM, N_KV_HEAD * DV), dtype=jnp.float32) * scale_in
        wo = jax.random.normal(ks[4], (N_HEAD * DV, DIM), dtype=jnp.float32) * scale_in
        return {'x': x, 'wq': wq, 'wk': wk, 'wv': wv, 'wo': wo}
    _L1_attn_in = _L1_attn_setup()

    def _L1_ffn_setup():
        import jax, jax.numpy as jnp
        import numpy as np
        TOP_K = 2
        SCALING = 2.0
        key = jax.random.key(seed)
        ks = jax.random.split(key, 10)
        B, S, H, I, E, R = (1, 64, 256, 128, 8, 16)
        w = 1.0 / np.sqrt(H)
        inp = {'x': jax.random.normal(ks[0], (B, S, H), jnp.float32), 'gate_weight': jax.random.normal(ks[1], (E, H), jnp.float32) * w, 'gate_lora_A': jax.random.normal(ks[2], (R, H), jnp.float32) * 0.02, 'gate_lora_B': jax.random.normal(ks[3], (E, R), jnp.float32) * 0.02, 'gate_up_proj': jax.random.normal(ks[4], (E, H, 2 * I), jnp.float32) * w, 'down_proj': jax.random.normal(ks[5], (E, I, H), jnp.float32) * (1.0 / np.sqrt(I)), 'gup_lora_A': jax.random.normal(ks[6], (E, R, H), jnp.float32) * 0.02, 'gup_lora_B': jax.random.normal(ks[7], (E, 2 * I, R), jnp.float32) * 0.02, 'down_lora_A': jax.random.normal(ks[8], (E, R, I), jnp.float32) * 0.02, 'down_lora_B': jax.random.normal(ks[9], (E, H, R), jnp.float32) * 0.02}
        return inp
    _L1_ffn_in = _L1_ffn_setup()
    _d = {'L0_attn_x': _L0_attn_in['x'], 'L0_attn_w_qkv': _L0_attn_in['w_qkv'], 'L0_attn_w_o': _L0_attn_in['w_o'], 'L0_attn_qn_g': _L0_attn_in['qn_g'], 'L0_attn_qn_b': _L0_attn_in['qn_b'], 'L0_attn_kn_g': _L0_attn_in['kn_g'], 'L0_attn_kn_b': _L0_attn_in['kn_b'], 'L0_ffn_ln_w': _L0_ffn_in['ln_w'], 'L0_ffn_ff_ln_w': _L0_ffn_in['ff_ln_w'], 'L0_ffn_wq': _L0_ffn_in['wq'], 'L0_ffn_wk': _L0_ffn_in['wk'], 'L0_ffn_wv': _L0_ffn_in['wv'], 'L0_ffn_wo': _L0_ffn_in['wo'], 'L0_ffn_gate_w': _L0_ffn_in['gate_w'], 'L0_ffn_w1': _L0_ffn_in['w1'], 'L0_ffn_w3': _L0_ffn_in['w3'], 'L0_ffn_w2': _L0_ffn_in['w2'], 'L1_attn_wq': _L1_attn_in['wq'], 'L1_attn_wk': _L1_attn_in['wk'], 'L1_attn_wv': _L1_attn_in['wv'], 'L1_attn_wo': _L1_attn_in['wo'], 'L1_ffn_gate_weight': _L1_ffn_in['gate_weight'], 'L1_ffn_gate_lora_A': _L1_ffn_in['gate_lora_A'], 'L1_ffn_gate_lora_B': _L1_ffn_in['gate_lora_B'], 'L1_ffn_gate_up_proj': _L1_ffn_in['gate_up_proj'], 'L1_ffn_down_proj': _L1_ffn_in['down_proj'], 'L1_ffn_gup_lora_A': _L1_ffn_in['gup_lora_A'], 'L1_ffn_gup_lora_B': _L1_ffn_in['gup_lora_B'], 'L1_ffn_down_lora_A': _L1_ffn_in['down_lora_A'], 'L1_ffn_down_lora_B': _L1_ffn_in['down_lora_B']}
    _x0 = _d['L0_attn_x']
    _d['L0_attn_x'] = jax.random.normal(jax.random.fold_in(jax.random.key(seed), 1), (1, 1024, 256), dtype=_x0.dtype)
    del _x0
    return _d

def reference(L0_attn_x, L0_attn_w_qkv, L0_attn_w_o, L0_attn_qn_g, L0_attn_qn_b, L0_attn_kn_g, L0_attn_kn_b, L0_ffn_ln_w, L0_ffn_ff_ln_w, L0_ffn_wq, L0_ffn_wk, L0_ffn_wv, L0_ffn_wo, L0_ffn_gate_w, L0_ffn_w1, L0_ffn_w3, L0_ffn_w2, L1_attn_wq, L1_attn_wk, L1_attn_wv, L1_attn_wo, L1_ffn_gate_weight, L1_ffn_gate_lora_A, L1_ffn_gate_lora_B, L1_ffn_gate_up_proj, L1_ffn_down_proj, L1_ffn_gup_lora_A, L1_ffn_gup_lora_B, L1_ffn_down_lora_A, L1_ffn_down_lora_B):

    def _L0_attn_ref(x, w_qkv, w_o, qn_g, qn_b, kn_g, kn_b):
        import jax, jax.numpy as jnp
        import numpy as np
        B, S, HID = (2, 256, 256)
        H, HKV, D = (16, 4, 128)
        ROPE_BASE = 1000000.0
        EPS = 1e-05

        def _layernorm(x, g, b):
            mu = jnp.mean(x, axis=-1, keepdims=True)
            var = jnp.mean(jnp.square(x - mu), axis=-1, keepdims=True)
            return (x - mu) * jax.lax.rsqrt(var + EPS) * g + b

        def _rope_tables(seq_len, dim, base):
            inv_freq = 1.0 / base ** (jnp.arange(0, dim, 2, dtype=jnp.float32) / dim)
            t = jnp.arange(seq_len, dtype=jnp.float32)
            freqs = jnp.outer(t, inv_freq)
            cos = jnp.concatenate([jnp.cos(freqs), jnp.cos(freqs)], axis=-1)
            sin = jnp.concatenate([jnp.sin(freqs), jnp.sin(freqs)], axis=-1)
            return (cos, sin)

        def _rotate_half(x):
            x1, x2 = jnp.split(x, 2, axis=-1)
            return jnp.concatenate([-x2, x1], axis=-1)
        b, s, _ = x.shape
        qkv = jnp.einsum('bsh,oh->bso', x, w_qkv)
        q, k, v = jnp.split(qkv, [H * D, (H + HKV) * D], axis=-1)
        q = q.reshape(b, s, H, D).transpose(0, 2, 1, 3)
        k = k.reshape(b, s, HKV, D).transpose(0, 2, 1, 3)
        v = v.reshape(b, s, HKV, D).transpose(0, 2, 1, 3)
        q = _layernorm(q, qn_g, qn_b)
        k = _layernorm(k, kn_g, kn_b)
        cos, sin = _rope_tables(s, D, ROPE_BASE)
        q = q * cos + _rotate_half(q) * sin
        k = k * cos + _rotate_half(k) * sin
        rep = H // HKV
        k = jnp.repeat(k, rep, axis=1)
        v = jnp.repeat(v, rep, axis=1)
        scores = jnp.einsum('bhqd,bhkd->bhqk', q, k) / jnp.sqrt(jnp.float32(D))
        causal = jnp.triu(jnp.ones((s, s), dtype=bool), k=1)
        scores = jnp.where(causal, -jnp.inf, scores)
        weights = jax.nn.softmax(scores, axis=-1)
        attn = jnp.einsum('bhqk,bhkd->bhqd', weights, v)
        attn = attn.transpose(0, 2, 1, 3).reshape(b, s, H * D)
        return jnp.einsum('bsd,od->bso', attn, w_o)

    def _L0_ffn_ref(x, ln_w, ff_ln_w, wq, wk, wv, wo, gate_w, w1, w3, w2):
        import jax, jax.numpy as jnp
        import numpy as np
        import math
        B, S, D = (2, 128, 256)
        H, KVH, HD = (16, 4, 128)
        E, K, FF = (8, 2, 896)
        EPS = 1e-05
        ROPE_BASE = 1000000.0

        def rmsnorm(x, w, eps=EPS):
            xf = x.astype(jnp.float32)
            var = jnp.mean(xf * xf, axis=-1, keepdims=True)
            return (xf * jax.lax.rsqrt(var + eps)).astype(x.dtype) * w

        def apply_rope(x, cos, sin):
            x1 = x[..., 0::2]
            x2 = x[..., 1::2]
            r1 = x1 * cos - x2 * sin
            r2 = x1 * sin + x2 * cos
            return jnp.stack([r1, r2], axis=-1).reshape(x.shape)
        Bx, Sx, Dx = x.shape
        residual = x
        h = rmsnorm(x, ln_w)
        q = (h @ wq).reshape(Bx, Sx, H, HD)
        k = (h @ wk).reshape(Bx, Sx, KVH, HD)
        v = (h @ wv).reshape(Bx, Sx, KVH, HD)
        pos = jnp.arange(Sx, dtype=jnp.float32)
        inv_freq = ROPE_BASE ** (-jnp.arange(0, HD, 2, dtype=jnp.float32) / HD)
        ang = pos[:, None] * inv_freq[None, :]
        cos = jnp.cos(ang)[None, :, None, :]
        sin = jnp.sin(ang)[None, :, None, :]
        q = apply_rope(q, cos, sin)
        k = apply_rope(k, cos, sin)
        rep = H // KVH
        k = jnp.repeat(k, rep, axis=2)
        v = jnp.repeat(v, rep, axis=2)
        scores = jnp.einsum('bqhd,bkhd->bhqk', q, k) / math.sqrt(HD)
        causal = jnp.tril(jnp.ones((Sx, Sx), dtype=bool))
        scores = jnp.where(causal[None, None], scores, jnp.finfo(scores.dtype).min)
        attn = jax.nn.softmax(scores, axis=-1)
        o = jnp.einsum('bhqk,bkhd->bqhd', attn, v).reshape(Bx, Sx, H * HD)
        x = o @ wo + residual
        residual = x
        h = rmsnorm(x, ff_ln_w)
        ht = h.reshape(-1, Dx)
        logits = ht @ gate_w
        top_vals, top_idx = jax.lax.top_k(logits, K)
        gates = jax.nn.softmax(top_vals, axis=-1)
        out = jnp.zeros_like(ht)
        for e in range(E):
            we = jnp.sum(gates * (top_idx == e), axis=-1)
            ye = jax.nn.silu(ht @ w1[e]) * (ht @ w3[e]) @ w2[e]
            out = out + we[:, None] * ye
        return out.reshape(Bx, Sx, Dx) + residual

    def _L1_attn_ref(x, wq, wk, wv, wo):
        import jax, jax.numpy as jnp
        import numpy as np
        DIM = 256
        N_HEAD = 16
        N_KV_HEAD = 4
        DQK = 128
        DV = DIM // N_HEAD
        N_REP = N_HEAD // N_KV_HEAD
        WIN = 64
        FRONT = 32
        SEQ = 512
        THETA = 10000.0

        def rope_cos_sin(seq_len, dim, theta=THETA):
            inv_freq = 1.0 / theta ** (np.arange(0, dim, 2)[:dim // 2].astype(np.float32) / dim)
            t = np.arange(seq_len, dtype=np.float32)
            ang = np.outer(t, inv_freq)
            return (jnp.asarray(np.cos(ang)), jnp.asarray(np.sin(ang)))

        def apply_rope(x, cos, sin):
            xr = x[..., 0::2]
            xi = x[..., 1::2]
            c = cos[None, :, None, :]
            s = sin[None, :, None, :]
            out_r = xr * c - xi * s
            out_i = xr * s + xi * c
            return jnp.stack([out_r, out_i], axis=-1).reshape(x.shape)

        def build_mask(seq_len, window, front):
            i = jnp.arange(seq_len)[:, None]
            j = jnp.arange(seq_len)[None, :]
            band = (j <= i) & (j > i - window)
            front_ok = (j < front) & (j <= i - window)
            allowed = band | front_ok
            return jnp.where(allowed, 0.0, -jnp.inf).astype(jnp.float32)
        B, S, _ = x.shape
        q = (x @ wq).reshape(B, S, N_HEAD, DQK)
        k = (x @ wk).reshape(B, S, N_KV_HEAD, DQK)
        v = (x @ wv).reshape(B, S, N_KV_HEAD, DV)
        cos, sin = rope_cos_sin(S, DQK)
        q = apply_rope(q, cos, sin)
        k = apply_rope(k, cos, sin)
        q = q.transpose(0, 2, 1, 3)
        k = k.transpose(0, 2, 1, 3)
        v = v.transpose(0, 2, 1, 3)
        k = jnp.repeat(k, N_REP, axis=1)
        v = jnp.repeat(v, N_REP, axis=1)
        mask = build_mask(S, WIN, FRONT)
        scores = jnp.einsum('bhqd,bhkd->bhqk', q, k) / np.sqrt(DQK).astype(np.float32)
        scores = scores + mask[None, None, :, :]
        attn = jax.nn.softmax(scores, axis=-1)
        out = jnp.einsum('bhqk,bhkd->bhqd', attn, v)
        out = out.transpose(0, 2, 1, 3).reshape(B, S, N_HEAD * DV)
        return out @ wo

    def _L1_ffn_ref(x, gate_weight, gate_lora_A, gate_lora_B, gate_up_proj, down_proj, gup_lora_A, gup_lora_B, down_lora_A, down_lora_B):
        import jax, jax.numpy as jnp
        import numpy as np
        TOP_K = 2
        SCALING = 2.0
        B, S, H = x.shape
        xf = x.reshape(-1, H)
        gate_delta = SCALING * (gate_lora_B @ gate_lora_A)
        router_logits = xf @ gate_weight.T + xf @ gate_delta.T
        probs = jax.nn.softmax(router_logits.astype(jnp.float32), axis=-1)
        routing_weights, selected = jax.lax.top_k(probs, TOP_K)
        routing_weights = routing_weights / routing_weights.sum(-1, keepdims=True)
        routing_weights = routing_weights.astype(xf.dtype)
        gup = jnp.einsum('th,eho->teo', xf, gate_up_proj)
        gup = gup + SCALING * jnp.einsum('ter,eor->teo', jnp.einsum('th,erh->ter', xf, gup_lora_A), gup_lora_B)
        gates, h = jnp.split(gup, 2, axis=-1)
        h = jax.nn.silu(gates) * h
        out = jnp.einsum('tei,eih->teh', h, down_proj)
        out = out + SCALING * jnp.einsum('ter,ehr->teh', jnp.einsum('tei,eri->ter', h, down_lora_A), down_lora_B)
        out_sel = jnp.take_along_axis(out, selected[:, :, None], axis=1)
        y = jnp.einsum('tkh,tk->th', out_sel, routing_weights)
        return y.reshape(B, S, H)
    x = L0_attn_x
    xn = _layernorm(x, axis=-1)
    s = _L0_attn_ref(xn, L0_attn_w_qkv, L0_attn_w_o, L0_attn_qn_g, L0_attn_qn_b, L0_attn_kn_g, L0_attn_kn_b)
    g = _silu(_L0_ffn_ref(xn, L0_ffn_ln_w, L0_ffn_ff_ln_w, L0_ffn_wq, L0_ffn_wk, L0_ffn_wv, L0_ffn_wo, L0_ffn_gate_w, L0_ffn_w1, L0_ffn_w3, L0_ffn_w2))
    x = x + s * g
    xn = _layernorm(x, axis=-1)
    s = _L1_attn_ref(xn, L1_attn_wq, L1_attn_wk, L1_attn_wv, L1_attn_wo)
    g = _silu(_L1_ffn_ref(xn, L1_ffn_gate_weight, L1_ffn_gate_lora_A, L1_ffn_gate_lora_B, L1_ffn_gate_up_proj, L1_ffn_down_proj, L1_ffn_gup_lora_A, L1_ffn_gup_lora_B, L1_ffn_down_lora_A, L1_ffn_down_lora_B))
    x = x + s * g
    return x

_drawn_inputs = setup_inputs


def setup_inputs(seed=0):
    import zlib

    import numpy as np

    out = dict(_drawn_inputs(seed))
    spreads = {'L0_attn_qn_g': (1.0, 0.6),
     'L0_attn_qn_b': (0.0, 0.8),
     'L0_attn_kn_g': (1.0, 0.6),
     'L0_attn_kn_b': (0.0, 0.8),
     'L0_ffn_ln_w': (1.0, 0.6),
     'L0_ffn_ff_ln_w': (1.0, 0.6)}
    factors = {'L0_ffn_wq': 8.0,
     'L0_ffn_wk': 8.0,
     'L0_ffn_wv': 8.0,
     'L0_ffn_wo': 8.0,
     'L0_ffn_gate_w': 8.0,
     'L0_ffn_w1': 8.0,
     'L0_ffn_w3': 8.0,
     'L0_ffn_w2': 8.0,
     'L1_ffn_gate_lora_A': 8.0,
     'L1_ffn_gate_lora_B': 8.0,
     'L1_ffn_gup_lora_A': 8.0,
     'L1_ffn_gup_lora_B': 8.0,
     'L1_ffn_down_lora_A': 8.0,
     'L1_ffn_down_lora_B': 8.0}
    for name, (base, spread) in spreads.items():
        noise = np.random.default_rng([zlib.crc32(name.encode()), seed]).standard_normal(out[name].shape)
        drawn = base * np.exp(spread * noise) if base else spread * noise
        out[name] = jnp.asarray(drawn.astype(out[name].dtype))
    for name, factor in factors.items():
        out[name] = (out[name] * factor).astype(out[name].dtype)
    return out
```

```python
from contextlib import ExitStack

import numpy as np

import concourse.bass as bass
from concourse import mybir

F32 = mybir.dt.float32
F32R = mybir.dt.float32r
BF16 = mybir.dt.bfloat16
U32 = mybir.dt.uint32
ALU = mybir.AluOpType
ACT = mybir.ActivationFunctionType
AX = mybir.AxisListType

P = 128
T = 1024
NT = T // P
HID = 256
KT = HID // P
H, HKV, D = 16, 4, 128
REP = H // HKV
NQK = H + HKV
QK = NQK * D
EPS = 1e-5
E = 8
FF = 896
FT = FF // P
DV1 = 16
I1 = 128
R1 = 16
NEG = -3.0e38
DEBUG = False


def split3(pe, out, wh, wl, xh, xl, start, stop):
    pe.matmul(out, wh, xh, start=start, stop=False)
    pe.matmul(out, wh, xl, start=False, stop=False)
    return pe.matmul(out, wl, xh, start=False, stop=stop)


class Scope:

    def __init__(self, nc, name):
        self.nc, self.name, self.stack, self.sems = nc, name, ExitStack(), []

    def __enter__(self):
        self.stack.__enter__()
        return self

    def __exit__(self, *a):
        self.stack.__exit__(*a)
        if self.sems:
            self.nc.clear_and_free_semaphores(self.sems)
            self.nc.all_engine_barrier()

    def sb(self, name, shape, dt=F32):
        return self.stack.enter_context(self.nc.sbuf_tensor(f"{self.name}_{name}", shape, dt))

    def ps(self, name, shape=(P, 512)):
        return self.stack.enter_context(self.nc.psum_tensor(f"{self.name}_{name}", list(shape), F32))

    def sem(self, name):
        self.sems.append(self.nc.alloc_semaphore(f"{self.name}_{name}"))
        return self.sems[-1]

    def block(self):
        return self.stack.enter_context(self.nc.Block())


def heads(ap, n):
    return ap.rearrange("p (h d) -> p h d", h=n)


def swapped(ap, n):
    return ap.rearrange("p (h s d) -> p h s d", h=n, s=2)[:, :, ::-1, :]


def load_stage(nc, G, a):
    with Scope(nc, "ld") as S:
        ld, ready = S.sem("ld"), S.sem("ready")
        block = S.block()

        @block.sync
        def _(sp):
            names = ("ident", "identb", "causal", "window0", "window")
            sp.dma_start(G["x"][:], a["x"].rearrange("(t p) d -> p t d", p=P)).then_inc(ld, 16)
            for n in names:
                sp.dma_start(G[n][:], a[n]).then_inc(ld, 16)
            sp.wait_ge(ld, 16 * (1 + len(names)))

        @block.gpsimd
        def _(pool):
            pool.memset(G["mhalf"][:], -0.5).then_inc(ready, 1)
            pool.wait_ge(ready, 1)


def prep_stage(nc, G, name, src, w, rope, qkT, vS, nv, rms=False, ln_w=None, gains=None, keep_xn=None):
    N = QK + nv
    NC = 6
    cw = [512] * 5 + [nv]
    with Scope(nc, name) as S:
        wh = S.sb("wh", [P, KT, N], F32R)
        wl = S.sb("wl", [P, KT, N], F32R)
        raw = S.sb("raw", [P, 2, QK])
        m1 = S.sb("m1", [P, 2, QK])
        m2 = S.sb("m2", [P, QK])
        qt = S.sb("qt", [P, 5, 512])
        vt = S.sb("vt", [P, nv])
        ntab = 2 if gains is not None else 4
        tab = S.sb("tab", [P, NT, ntab, D])
        xs = S.sb("xs", [P, 2, HID])
        xth = S.sb("xth", [P, 2, HID], F32R)
        xtl = S.sb("xtl", [P, 2, HID], F32R)
        st = S.sb("st", [P, 8])
        mv = S.sb("mv", [P, 2, 2])
        rstd = S.sb("rstd", [P, 2, 1])
        rin = S.sb("rin", [P, 2, 1])
        if ln_w is not None:
            lnw = S.sb("lnw", [P, KT])
        if gains is not None:
            gb = S.sb("gb", [P, 4, D])
            gt = S.sb("gt", [P, NT, 6, D])
            hst = S.sb("hst", [P, NQK, 6])
            hs = S.sb("hs", [P, 2, 6, NQK])
        psX = [S.ps(f"psX{i}") for i in range(2)]
        psJ = [S.ps(f"psJ{i}") for i in range(4)]
        psT = [S.ps(f"psT{i}") for i in range(2)]

        w_in, w_hi, w_lo = S.sem("w_in"), S.sem("w_hi"), S.sem("w_lo")
        tab_in, tabs = S.sem("tab_in"), S.sem("tabs")
        s_mv, s_rstd, s_xs = S.sem("mv"), S.sem("rstd"), S.sem("xs")
        s_xtr, s_xhi, s_xlo = S.sem("xtr"), S.sem("xhi"), S.sem("xlo")
        s_pj, s_raw = S.sem("pj"), S.sem("raw")
        s_var, s_hrs, s_nmr, s_xh = S.sem("var"), S.sem("hrs"), S.sem("nmr"), S.sem("xh")
        s_m, s_q, s_tr, s_qt = S.sem("m"), S.sem("q"), S.sem("tr"), S.sem("qt")
        s_qst, s_vst = [S.sem(f"qst{b}") for b in range(5)], S.sem("vst")
        s_fin = s_q if gains is not None else s_m
        slab = [raw[:].rearrange("p u n -> p (u n)")[:, 0:N], m1[:].rearrange("p u n -> p (u n)")[:, 0:N]]
        block = S.block()

        def tiles(eng, step):
            step(None, 0, 1)
            step(0, 1, 0)
            with eng.Fori(0, 3) as i:
                step(i * 2 + 1, i * 2 + 2, 1)
                step(i * 2 + 2, i * 2 + 3, 0)
            step(NT - 1, None, 1)


        @block.sync
        def _(sp):
            for k in range(KT):
                sp.dma_start(slab[k], w[k * P:(k + 1) * P, :]).then_inc(w_in, 16)
            sp.dma_start(tab[:], rope.rearrange("(t p) c d -> p t c d", p=P)).then_inc(tab_in, 16)
            if gains is not None:
                for j, g in enumerate(gains):
                    sp.dma_start(gb[:, j, :], g.rearrange("(o d) -> o d", o=1).broadcast_to([P, D])).then_inc(tab_in, 16)
            if ln_w is not None:
                sp.dma_start(lnw[:], ln_w).then_inc(tab_in, 16)

            def step(tb, tf, ub):
                if tb is not None:
                    sp.wait_ge(s_raw, 6 * tb + 6)
                    sp.dma_start(vS[:, bass.ds(tb, 1), :].rearrange("p o n -> p (o n)"), vt[:]).then_inc(s_vst, 16)
                    for b in range(5):
                        sp.wait_ge(s_qt, 5 * tb + b + 1)
                        sp.dma_start(qkT[:, bass.ds(tb, 1), b * 512:(b + 1) * 512].rearrange("p o n -> p (o n)"),
                                     qt[:, b, :]).then_inc(s_qst[b], 16)
            tiles(sp, step)
            for b in range(5):
                sp.wait_ge(s_qst[b], 16 * NT)
            sp.wait_ge(s_vst, 16 * NT)

        @block.tensor
        def _(pe):
            pe.wait_ge(w_lo, KT)

            def step(tb, tf, ub):
                uf = 1 - ub
                if tf is not None:
                    pe.wait_ge(s_xs, tf + 1)
                    if not (isinstance(tf, int) and tf < 2):
                        pe.wait_ge(s_xlo, tf - 1)
                    for k in range(KT):
                        mm = pe.transpose(psX[uf][:, k * P:(k + 1) * P], xs[:, uf, k * P:(k + 1) * P], G["ident"][:])
                    mm.then_inc(s_xtr, 1)
                    pe.wait_ge(s_xlo, tf + 1)
                    for c in range(NC):
                        if not (isinstance(tf, int) and 6 * tf + c < 4):
                            pe.wait_ge(s_raw, 6 * tf + c - 3)
                        out = psJ[(6 * uf + c) % 4][:, 0:cw[c]]
                        for k in range(KT):
                            mm = split3(pe, out, xth[:, uf, k * P:(k + 1) * P], xtl[:, uf, k * P:(k + 1) * P],
                                        wh[:, k, c * 512:c * 512 + cw[c]], wl[:, k, c * 512:c * 512 + cw[c]],
                                        k == 0, k == KT - 1)
                        mm.then_inc(s_pj, 1)
                if tb is not None:
                    pe.wait_ge(s_fin, tb + 1)
                    for b in range(5):
                        if not (isinstance(tb, int) and 5 * tb + b < 2):
                            pe.wait_ge(s_qt, 5 * tb + b - 1)
                        for j in range(4):
                            h = 4 * b + j
                            mm = pe.transpose(psT[(5 * ub + b) % 2][:, j * P:(j + 1) * P],
                                              m1[:, ub, h * D:(h + 1) * D], G["ident"][:])
                        mm.then_inc(s_tr, 1)
            tiles(pe, step)

        @block.scalar
        def _(act):
            for k in range(KT):
                act.wait_ge(w_in, 16 * KT)
                act.activation(wh[:, k, :], slab[k], ACT.Copy).then_inc(w_hi, 1)
            if ln_w is not None:
                act.wait_ge(tab_in, 32)
            act.wait_ge(w_lo, KT)

            def step(tb, tf, ub):
                uf = 1 - ub
                if tf is not None:
                    if not (isinstance(tf, int) and tf < 2):
                        act.wait_ge(s_pj, 6 * (tf - 1))
                    act.wait_ge(s_xtr, tf + 1)
                    if ln_w is None:
                        act.activation(xth[:, uf, :], psX[uf][:, 0:HID], ACT.Copy).then_inc(s_xhi, 1)
                    else:
                        for k in range(KT):
                            i = act.activation(xth[:, uf, k * P:(k + 1) * P], psX[uf][:, k * P:(k + 1) * P],
                                               ACT.Copy, scale=lnw[:, k:k + 1])
                        i.then_inc(s_xhi, 1)
                if tb is not None and gains is not None:
                    act.wait_ge(s_nmr, tb + 1)
                    for h in range(NQK):
                        i = act.activation(raw[:, ub, h * D:(h + 1) * D], raw[:, ub, h * D:(h + 1) * D], ACT.Identity,
                                           scale=hs[:, ub, 4, h:h + 1], bias=hs[:, ub, 5, h:h + 1])
                    i.then_inc(s_xh, 1)
                if tf is not None:
                    if not (isinstance(tf, int) and tf < 2):
                        act.wait_ge(s_m, tf - 1)
                    for c in range(NC):
                        act.wait_ge(s_pj, 6 * tf + c + 1)
                        if c == 5 and not (isinstance(tf, int) and tf < 1):
                            act.wait_ge(s_vst, 16 * tf)
                        dst = raw[:, uf, c * 512:(c + 1) * 512] if c < 5 else vt[:]
                        act.activation(dst, psJ[(6 * uf + c) % 4][:, 0:cw[c]], ACT.Copy).then_inc(s_raw, 1)
                if tb is not None:
                    for b in range(5):
                        act.wait_ge(s_tr, 5 * tb + b + 1)
                        if not (isinstance(tb, int) and tb < 1):
                            act.wait_ge(s_qst[b], 16 * tb)
                        act.activation(qt[:, b, :], psT[(5 * ub + b) % 2][:], ACT.Copy).then_inc(s_qt, 1)
            tiles(act, step)

        @block.vector
        def _(dve):
            for k in range(KT):
                dve.wait_ge(w_hi, k + 1)
                dve.tensor_tensor(wl[:, k, :], slab[k], wh[:, k, :].bitcast(F32), ALU.subtract).then_inc(w_lo, 1)
            dve.wait_ge(tab_in, 16 * (1 + (4 if gains is not None else 0) + (1 if ln_w is not None else 0)))
            if gains is not None:
                for j in range(2):
                    scale = float(D) ** -0.5 if j == 0 else 1.0
                    g = gb[:, j, :].rearrange("p (o d) -> p o d", o=1).broadcast_to([P, NT, D])
                    b = gb[:, 2 + j, :].rearrange("p (o d) -> p o d", o=1).broadcast_to([P, NT, D])
                    if j == 0:
                        dve.tensor_scalar(gb[:, 0, :], gb[:, 0, :], scale, None, ALU.mult)
                        dve.tensor_scalar(gb[:, 2, :], gb[:, 2, :], scale, None, ALU.mult)
                        dve.drain()
                    dve.tensor_tensor(gt[:, :, 3 * j, :], tab[:, :, 0, :], g, ALU.mult)
                    dve.tensor_tensor(gt[:, :, 3 * j + 2, :], tab[:, :, 0, :], b, ALU.mult)
                    for s in range(2):
                        o = slice(s * 64, s * 64 + 64)
                        r = slice(64 - s * 64, 128 - s * 64)
                        dve.tensor_tensor(gt[:, :, 3 * j + 1, o], tab[:, :, 1, o], g[:, :, r], ALU.mult)
                        dve.drain()
                        dve.tensor_tensor(m2[:, 0:NT * 64].rearrange("p (t d) -> p t d", t=NT), tab[:, :, 1, o],
                                          b[:, :, r], ALU.mult)
                        dve.drain()
                        dve.tensor_tensor(gt[:, :, 3 * j + 2, o], gt[:, :, 3 * j + 2, o],
                                          m2[:, 0:NT * 64].rearrange("p (t d) -> p t d", t=NT), ALU.add)
                dve.drain().then_inc(tabs, 1)
            dve.wait_ge(w_lo, KT)

            def table(t, j):
                src_tab = gt if gains is not None else tab
                return src_tab[:, bass.ds(t, 1), j, :]

            def step(tb, tf, ub):
                uf = 1 - ub
                if tb is not None and gains is not None:
                    dve.wait_ge(s_raw, 6 * tb + 5)
                    for h in range(NQK):
                        dve.bn_stats(hst[:, h, :], raw[:, ub, h * D:(h + 1) * D])
                    dve.drain()
                    ev, od = 0, 3
                    h6 = hst[:].rearrange("p h s -> p s h")
                    dve.tensor_tensor(hs[:, ub, 0, :], h6[:, ev + 1, :], h6[:, od + 1, :], ALU.add)
                    dve.tensor_tensor(hs[:, ub, 1, :], h6[:, ev + 1, :], h6[:, od + 1, :], ALU.subtract)
                    dve.tensor_tensor(hs[:, ub, 2, :], h6[:, ev + 2, :], h6[:, od + 2, :], ALU.add)
                    dve.drain()
                    dve.tensor_tensor(hs[:, ub, 1, :], hs[:, ub, 1, :], hs[:, ub, 1, :], ALU.mult)
                    dve.drain()
                    dve.scalar_tensor_tensor(hs[:, ub, 3, :], hs[:, ub, 1, :], D / 4.0, hs[:, ub, 2, :],
                                             ALU.mult, ALU.add)
                    dve.drain()
                    dve.tensor_scalar(hs[:, ub, 3, :], hs[:, ub, 3, :], 1.0 / D, EPS, ALU.mult, ALU.add).then_inc(s_var, 1)
                if tf is not None:
                    x = src[:, bass.ds(tf, 1), :].rearrange("p o d -> p (o d)")
                    dve.bn_stats(st[:, 0:6], x)
                    dve.drain()
                    dve.bn_aggr(mv[:, uf, :], st[:, 0:6])
                    dve.drain()
                    if rms:
                        dve.scalar_tensor_tensor(mv[:, uf, 1:2], mv[:, uf, 0:1], mv[:, uf, 0:1], mv[:, uf, 1:2],
                                                 ALU.mult, ALU.add)
                        dve.drain()
                    dve.tensor_scalar(rin[:, uf, :], mv[:, uf, 1:2], EPS, None, ALU.add).then_inc(s_mv, 1)
                    dve.wait_ge(s_rstd, tf + 1)
                    if not (isinstance(tf, int) and tf < 2):
                        dve.wait_ge(s_xtr, tf - 1)
                    if rms:
                        dve.tensor_scalar(xs[:, uf, :], x, rstd[:, uf, :], None, ALU.mult).then_inc(s_xs, 1)
                    else:
                        dve.tensor_scalar(xs[:, uf, :], x, mv[:, uf, 0:1], rstd[:, uf, :], ALU.subtract,
                                          ALU.mult).then_inc(s_xs, 1)
                    if keep_xn is not None:
                        dve.drain()
                        dve.tensor_copy(keep_xn[:, bass.ds(tf, 1), :].rearrange("p o d -> p (o d)"), xs[:, uf, :])
                    if tb is not None and gains is not None:
                        neg_mean(tb, ub)
                    dve.wait_ge(s_xhi, tf + 1)
                    if ln_w is None:
                        dve.tensor_tensor(xtl[:, uf, :], psX[uf][:, 0:HID], xth[:, uf, :].bitcast(F32),
                                          ALU.subtract).then_inc(s_xlo, 1)
                    else:
                        for k in range(KT):
                            ks = slice(k * P, (k + 1) * P)
                            i = dve.scalar_tensor_tensor(xtl[:, uf, ks], psX[uf][:, ks], lnw[:, k:k + 1],
                                                         xth[:, uf, ks].bitcast(F32), ALU.mult, ALU.subtract)
                        i.then_inc(s_xlo, 1)
                elif gains is not None:
                    neg_mean(tb, ub)
                if tb is not None:
                    if gains is not None:
                        dve.wait_ge(s_xh, tb + 1)
                    else:
                        dve.wait_ge(s_raw, 6 * tb + 5)
                    if not (isinstance(tb, int) and tb < 2):
                        dve.wait_ge(s_tr, 5 * (tb - 1))
                    if not (isinstance(tb, int) and tb < 1):
                        dve.wait_ge(s_m, tb)
                    nt3 = 3 if gains is not None else 2
                    for j, (a, n) in enumerate(((0, H), (H, HKV))):
                        c = slice(a * D, (a + n) * D)
                        cos = table(tb, nt3 * j).broadcast_to([P, n, D])
                        dve.tensor_tensor(heads(m1[:, ub, c], n), heads(raw[:, ub, c], n), cos, ALU.mult)
                        sin = table(tb, nt3 * j + 1).rearrange("p o (s d) -> p o s d", s=2).broadcast_to([P, n, 2, 64])
                        dve.tensor_tensor(m2[:, c].rearrange("p (h s d) -> p h s d", h=n, s=2), swapped(raw[:, ub, c], n),
                                          sin, ALU.mult)
                    dve.drain()
                    dve.tensor_tensor(m1[:, ub, :], m1[:, ub, :], m2[:], ALU.add).then_inc(s_m, 1)

            def neg_mean(tb, ub):
                dve.wait_ge(s_hrs, tb + 1)
                dve.scalar_tensor_tensor(hs[:, ub, 5, :], hs[:, ub, 0, :], -0.5, hs[:, ub, 4, :],
                                         ALU.mult, ALU.mult).then_inc(s_nmr, 1)
            tiles(dve, step)

        @block.gpsimd
        def _(pool):
            if gains is not None:
                pool.wait_ge(tabs, 1)

            def step(tb, tf, ub):
                uf = 1 - ub
                if tb is not None and gains is not None:
                    pool.wait_ge(s_var, tb + 1)
                    pool.tensor_tensor(hs[:, ub, 4, :], hs[:, ub, 3, :], G["mhalf"][:, 0:NQK], ALU.pow).then_inc(s_hrs, 1)
                if tf is not None:
                    pool.wait_ge(s_mv, tf + 1)
                    if not (isinstance(tf, int) and tf < 2):
                        pool.wait_ge(s_xs, tf - 1)
                    pool.tensor_tensor(rstd[:, uf, :], rin[:, uf, :], G["mhalf"][:, 0:1], ALU.pow).then_inc(s_rstd, 1)
                if tb is not None and gains is not None:
                    pool.wait_ge(s_m, tb + 1)
                    for j, (a, n) in enumerate(((0, H), (H, HKV))):
                        c = slice(a * D, (a + n) * D)
                        bias = gt[:, bass.ds(tb, 1), 3 * j + 2, :].broadcast_to([P, n, D])
                        i = pool.tensor_tensor(heads(m1[:, ub, c], n), heads(m1[:, ub, c], n), bias, ALU.add)
                    i.then_inc(s_q, 1)
            tiles(pool, step)


def attention_stage(nc, G, name, qkT, vS, oT, rS):
    with Scope(nc, name) as S:
        kv_raw = S.sb("kv_raw", [P, 2, T])
        kh, kl = S.sb("kh", [P, T], F32R), S.sb("kl", [P, T], F32R)
        vh, vl = S.sb("vh", [P, T], F32R), S.sb("vl", [P, T], F32R)
        q_raw = S.sb("q_raw", [P, 2, T])
        qh, ql = S.sb("qh", [P, 2, T], F32R), S.sb("ql", [P, 2, T], F32R)
        pr = S.sb("pr", [P, 3, T])
        pth = S.sb("pth", [P, 2, NT, 512], F32R)
        ptl = S.sb("ptl", [P, 2, NT, 512], F32R)
        ob = S.sb("ob", [P, 2, 512])
        nm = S.sb("nm", [P, 4])
        rs = S.sb("rs", [P, REP * NT])
        rall = S.sb("rall", [P, H * NT])
        rT = S.sb("rT", [P, P])
        psS = [S.ps(f"psS{i}", (P, 1024)) for i in range(2)]
        psP = [S.ps(f"psP{i}") for i in range(2)]
        psO = [S.ps(f"psO{i}") for i in range(2)]

        kv_in, kv_hi, kv_lo = S.sem("kv_in"), S.sem("kv_hi"), S.sem("kv_lo")
        q_in, q_hi, q_lo = [S.sem("q_in0"), S.sem("q_in1")], S.sem("q_hi"), S.sem("q_lo")
        scores, negmax, probs = S.sem("scores"), S.sem("negmax"), S.sem("probs")
        turned, pt_hi, pt_lo = S.sem("turned"), S.sem("pt_hi"), S.sem("pt_lo")
        pv, o_out, o_st = S.sem("pv"), S.sem("o_out"), [S.sem("o_st0"), S.sem("o_st1")]
        recip, r_tr, r_sb, r_st = S.sem("recip"), S.sem("r_tr"), S.sem("r_sb"), S.sem("r_st")

        STEPS = REP * NT
        nb = [(t // 4) + 1 for t in range(NT)]
        BH = sum(nb)
        bstart = [sum(nb[:t]) for t in range(NT)]
        BR = REP * BH

        def batch(s):
            return (s // NT) * BH + bstart[s % NT]

        block = S.block()
        r3 = lambda ap: ap.rearrange("p (t n) -> p t n", t=NT)

        def store_o(sp, g, j):
            for half in range(2):
                sp.wait_ge(o_out, (g * REP + j) * 2 + half + 1)
                dst = oT[:, 4 * half:4 * half + 4, bass.ds(g * (REP * D) + j * D, D)]
                sp.dma_start(dst, ob[:, half, :].rearrange("p (t n) -> p t n", t=4)).then_inc(o_st[half], 16)

        @block.sync
        def _(sp):
            def load_q(g, j):
                h = g * REP + j
                sp.dma_start(r3(q_raw[:, j % 2, :]), qkT[:, :, bass.ds(h * D, D)]).then_inc(q_in[j % 2], 16)

            with sp.Fori(0, HKV) as g:
                sp.wait_ge(kv_lo, g * 2)
                sp.dma_start(r3(kv_raw[:, 0, :]), qkT[:, :, bass.ds(g * D + H * D, D)]).then_inc(kv_in, 16)
                sp.dma_start(r3(kv_raw[:, 1, :]), vS[:, :, bass.ds(g * D, D)]).then_inc(kv_in, 16)
                for j in range(REP):
                    sp.wait_ge(q_lo, g * REP + max(0, j - 1))
                    load_q(g, j)
                    if j >= 1:
                        store_o(sp, g, j - 1)
                store_o(sp, g, REP - 1)
            sp.wait_ge(r_sb, 1)
            sp.dma_start(rS, rT[:]).then_inc(r_st, 16)
            sp.wait_ge(r_st, 16)
            for half in range(2):
                sp.wait_ge(o_st[half], 16 * H)

        @block.tensor
        def _(pe):
            def score(g, s):
                j, t = divmod(s, NT)
                n = (t + 1) * P
                if t == 0:
                    pe.wait_ge(q_lo, g * REP + j + 1)
                pe.wait_ge(probs, g * STEPS + max(0, s - 1))
                out = psS[s % 2]
                ql_, qh_ = ql[:, j % 2, t * P:(t + 1) * P], qh[:, j % 2, t * P:(t + 1) * P]
                for c in range(0, n, 512):
                    e = min(n, c + 512)
                    mm = split3(pe, out[:, c:e], qh_, ql_, kh[:, c:e], kl[:, c:e], True, e < n)
                mm = pe.matmul(out[:, n - P:n], G["identb"][:], G["causal"][:], start=False, stop=True)
                mm.then_inc(scores, 1)

            def turn(g, s):
                j, t = divmod(s, NT)
                pe.wait_ge(probs, g * STEPS + s + 1)
                for b in range(nb[t]):
                    i = batch(s) + b
                    pe.wait_ge(pt_lo, g * BR + max(0, i - 1))
                    for y in range(4 * b, min(4 * b + 4, t + 1)):
                        mm = pe.transpose(psP[i % 2][:, (y - 4 * b) * P:(y - 4 * b + 1) * P],
                                          pr[:, s % 3, y * P:(y + 1) * P], G["ident"][:])
                    mm.then_inc(turned, 1)

            def values(g, j, half):
                i = 2 * j + half
                last = j * NT + 4 * half + 3
                pe.wait_ge(pt_lo, g * BR + batch(last) + nb[last % NT])
                pe.wait_ge(o_out, g * 2 * REP + max(0, i - 1))
                ny = 4 * half + 4
                for y in range(ny):
                    q0 = max(0, y - 4 * half) * P
                    mm = split3(pe, psO[i % 2][:, q0:512], vh[:, y * P:(y + 1) * P], vl[:, y * P:(y + 1) * P],
                                pth[:, half, y, q0:512], ptl[:, half, y, q0:512], y == 0, y == ny - 1)
                mm.then_inc(pv, 1)

            with pe.Fori(0, HKV) as g:
                pe.wait_ge(kv_lo, g * 2 + 2)
                for s in range(STEPS + 4):
                    if s < STEPS:
                        score(g, s)
                    if 2 <= s < STEPS + 2:
                        turn(g, s - 2)
                    if s >= 3 and (s - 3) % 4 == 3 and s - 3 < STEPS:
                        values(g, (s - 3) // NT, ((s - 3) % NT) // 4)
            pe.wait_ge(recip, HKV)
            pe.transpose(psP[0][:, 0:P], rall[:], G["ident"][:]).then_inc(r_tr, 1)

        @block.scalar
        def _(act):
            def q_part(g, j):
                act.wait_ge(q_in[j % 2], 16 * (g * (REP // 2) + j // 2 + 1))
                act.wait_ge(scores, g * STEPS + max(0, (j - 1) * NT))
                act.activation(qh[:, j % 2, :], q_raw[:, j % 2, :], ACT.Copy).then_inc(q_hi, 1)

            def hi(g, s):
                j, t = divmod(s, NT)
                half, q = t // 4, (t % 4) * P
                if t % 4 == 0:
                    act.wait_ge(pv, g * 2 * REP + max(0, 2 * j + half - 1))
                for b in range(nb[t]):
                    i = batch(s) + b
                    n = min(4, t + 1 - 4 * b)
                    act.wait_ge(turned, g * BR + i + 1)
                    act.activation(pth[:, half, 4 * b:4 * b + n, q:q + P],
                                   psP[i % 2][:, 0:n * P].rearrange("p (y q) -> p y q", y=n), ACT.Copy).then_inc(pt_hi, 1)

            with act.Fori(0, HKV) as g:
                act.wait_ge(pv, g * 2 * REP)
                act.wait_ge(kv_in, g * 32 + 32)
                act.activation(kh[:], kv_raw[:, 0, :], ACT.Copy).then_inc(kv_hi, 1)
                act.activation(vh[:], kv_raw[:, 1, :], ACT.Copy).then_inc(kv_hi, 1)
                for s in range(STEPS + 2):
                    if s < STEPS and s % NT == 0 and s == 0:
                        q_part(g, 0)
                    if s % NT == NT - 3 and s // NT + 1 < REP:
                        q_part(g, s // NT + 1)
                    if s >= 2:
                        hi(g, s - 2)
                    if s < STEPS:
                        t = s % NT
                        act.wait_ge(negmax, g * STEPS + s + 1)
                        act.wait_ge(turned, g * BR + (batch(s - 3) + nb[(s - 3) % NT] if s >= 3 else 0))
                        if s == 0:
                            act.wait_ge(recip, g)
                        act.activation(pr[:, s % 3, 0:(t + 1) * P], psS[s % 2][:, 0:(t + 1) * P], ACT.Exp,
                                       bias=nm[:, s % 4:s % 4 + 1], accum_out=rs[:, s:s + 1]).then_inc(probs, 1)
            act.wait_ge(r_tr, 1)
            act.activation(rT[:], psP[0][:, 0:P], ACT.Copy).then_inc(r_sb, 1)

        @block.vector
        def _(dve):
            def q_part(g, j):
                dve.wait_ge(q_hi, g * REP + j + 1)
                dve.tensor_tensor(ql[:, j % 2, :], q_raw[:, j % 2, :], qh[:, j % 2, :].bitcast(F32),
                                  ALU.subtract).then_inc(q_lo, 1)

            def lo(g, s):
                j, t = divmod(s, NT)
                half, q = t // 4, (t % 4) * P
                for b in range(nb[t]):
                    i = batch(s) + b
                    n = min(4, t + 1 - 4 * b)
                    dve.wait_ge(pt_hi, g * BR + i + 1)
                    blk = (slice(None), half, slice(4 * b, 4 * b + n), slice(q, q + P))
                    dve.tensor_tensor(ptl[blk], psP[i % 2][:, 0:n * P].rearrange("p (y q) -> p y q", y=n),
                                      pth[blk].bitcast(F32), ALU.subtract).then_inc(pt_lo, 1)

            def out(g, j, half):
                i = 2 * j + half
                dve.wait_ge(pv, g * 2 * REP + i + 1)
                dve.wait_ge(o_st[half], g * (16 * REP) + 16 * j)
                dve.tensor_copy(ob[:, half, :], psO[i % 2][:]).then_inc(o_out, 1)

            with dve.Fori(0, HKV) as g:
                for k, (h, l) in enumerate(((kh, kl), (vh, vl))):
                    dve.wait_ge(kv_hi, g * 2 + k + 1)
                    dve.tensor_tensor(l[:], kv_raw[:, k, :], h[:].bitcast(F32), ALU.subtract).then_inc(kv_lo, 1)
                for s in range(STEPS + 5):
                    if s < STEPS and s == 0:
                        q_part(g, 0)
                    if s % NT == NT - 3 and s // NT + 1 < REP and s < STEPS:
                        q_part(g, s // NT + 1)
                    if s < STEPS:
                        t = s % NT
                        dve.wait_ge(scores, g * STEPS + s + 1)
                        dve.tensor_reduce(nm[:, s % 4:s % 4 + 1], psS[s % 2][:, 0:(t + 1) * P], AX.X, ALU.max,
                                          negate=True).then_inc(negmax, 1)
                    if 2 <= s < STEPS + 2:
                        lo(g, s - 2)
                    if s >= 4 and (s - 4) % 4 == 3 and s - 4 < STEPS:
                        out(g, (s - 4) // NT, ((s - 4) % NT) // 4)
                dve.wait_ge(probs, g * STEPS + STEPS)
                dve.reciprocal(rall[:, bass.ds(g * STEPS, STEPS)], rs[:]).then_inc(recip, 1)


def row(ap, t):
    return ap[:, bass.ds(t, 1), :].rearrange("p o n -> p (o n)")


def heads_out_stage(nc, G, name, projections):
    with Scope(nc, name) as S:
        wraw = S.sb("wraw", [P, H, HID])
        wh = [S.sb(f"wh{i}", [P, H, HID], F32R) for i in range(2)]
        wl = [S.sb(f"wl{i}", [P, H, HID], F32R) for i in range(2)]
        o = [S.sb(f"o{i}", [P, H * P]) for i in range(2)]
        r = [S.sb(f"r{i}", [P, H, P]) for i in range(2)]
        oh = [S.sb(f"oh{i}", [P, H * P], F32R) for i in range(2)]
        ol = [S.sb(f"ol{i}", [P, H * P], F32R) for i in range(2)]
        ps = [S.ps(f"ps{i}") for i in range(2)]
        w_in, w_hi, w_lo = S.sem("w_in"), S.sem("w_hi"), S.sem("w_lo")
        o_in = [S.sem(f"o_in{i}") for i in range(2)]
        scaled = [S.sem(f"scaled{i}") for i in range(2)]
        hi = [S.sem(f"hi{i}") for i in range(2)]
        lo = [S.sem(f"lo{i}") for i in range(2)]
        done = [S.sem(f"done{i}") for i in range(2)]
        out = [S.sem(f"out{i}") for i in range(2)]
        block = S.block()

        @block.sync
        def _(sp):
            def tile(t, i):
                oT, rS, _ = projections[i]
                sp.wait_ge(lo[i], t)
                sp.dma_start(o[i][:], row(oT, t)).then_inc(o_in[i], 16)
                rt = rS.rearrange("(o h t) q -> o h t q", o=1, h=H)[:, :, bass.ds(t, 1), :]
                sp.dma_start(r[i][:], rt.rearrange("o h u q -> o h (u q)").broadcast_to([P, H, P])).then_inc(o_in[i], 16)
            for i in range(2):
                sp.wait_ge(w_lo, i)
                sp.dma_start(wraw[:], projections[i][2].rearrange("(h p) n -> p h n", p=P)).then_inc(w_in, 16)
            with sp.Fori(0, NT) as t:
                for i in range(2):
                    tile(t, i)

        @block.tensor
        def _(pe):
            pe.wait_ge(w_lo, 2)
            with pe.Fori(0, NT) as t:
                for i in range(2):
                    pe.wait_ge(lo[i], t + 1)
                    pe.wait_ge(out[i], t)
                    for h in range(H):
                        hs = slice(h * P, (h + 1) * P)
                        mm = split3(pe, ps[i][:, 0:HID], oh[i][:, hs], ol[i][:, hs], wh[i][:, h, :], wl[i][:, h, :],
                                    h == 0, h == H - 1)
                    mm.then_inc(done[i], 1)

        @block.scalar
        def _(act):
            for i in range(2):
                act.wait_ge(w_in, 16 * (i + 1))
                act.activation(wh[i][:], wraw[:], ACT.Copy).then_inc(w_hi, 1)
            with act.Fori(0, NT) as t:
                for i in range(2):
                    act.wait_ge(scaled[i], t + 1)
                    act.wait_ge(done[i], t)
                    act.activation(oh[i][:], o[i][:], ACT.Copy).then_inc(hi[i], 1)

        @block.vector
        def _(dve):
            for i in range(2):
                dve.wait_ge(w_hi, i + 1)
                dve.tensor_tensor(wl[i][:], wraw[:], wh[i][:].bitcast(F32), ALU.subtract).then_inc(w_lo, 1)

            def scale(t, i):
                dve.wait_ge(o_in[i], t * 32 + 32)
                dve.tensor_tensor(o[i][:], o[i][:], r[i][:].rearrange("p h q -> p (h q)"), ALU.mult).then_inc(scaled[i], 1)

            def evacuate(t, i):
                dve.wait_ge(done[i], t + 1)
                if i == 0:
                    dve.tensor_copy(row(G["s"], t), ps[i][:, 0:HID]).then_inc(out[i], 1)
                else:
                    dve.tensor_tensor(row(G["x2"], t), ps[i][:, 0:HID], row(G["xn"], t), ALU.add).then_inc(out[i], 1)

            def low(t, i):
                dve.wait_ge(hi[i], t + 1)
                dve.tensor_tensor(ol[i][:], o[i][:], oh[i][:].bitcast(F32), ALU.subtract).then_inc(lo[i], 1)

            scale(0, 0)
            low(0, 0)
            scale(0, 1)
            low(0, 1)
            with dve.Fori(0, NT - 1) as t:
                for i in range(2):
                    scale(t + 1, i)
                    evacuate(t, i)
                    low(t + 1, i)
            for i in range(2):
                evacuate(NT - 1, i)


def rows_stage(nc, G, name, src, *, ln_w=None, keep=None, product=None, dst=None, gate=None, gate_sb=None, logits=None):
    with Scope(nc, name) as S:
        xs = S.sb("xs", [P, 2, HID])
        xt = S.sb("xt", [P, 2, HID])
        xh, xl = S.sb("xh", [P, 2, HID], F32R), S.sb("xl", [P, 2, HID], F32R)
        st, mv = S.sb("st", [P, 8]), S.sb("mv", [P, 2])
        rin, rstd = S.sb("rin", [P, 2]), S.sb("rstd", [P, 2])
        gw = gate_sb if gate_sb is not None else S.sb("gw", [P, KT, E])
        lnw = S.sb("lnw", [P, KT])
        psX = [S.ps(f"psX{i}") for i in range(2)]
        psY = [S.ps(f"psY{i}") for i in range(2)]
        w_in, w_hi, w_lo = S.sem("w_in"), S.sem("w_hi"), S.sem("w_lo")
        var, rs, normed = S.sem("var"), S.sem("rs"), S.sem("normed")
        turned, whole, high, low = S.sem("turned"), S.sem("whole"), S.sem("high"), S.sem("low")
        done, out = S.sem("done"), S.sem("out")
        if product is not None:
            wraw = S.sb("wraw", [P, KT, HID])
            wh, wl = S.sb("wh", [P, KT, HID], F32R), S.sb("wl", [P, KT, HID], F32R)
        n_in = 16 * ((product is not None) + (gate is not None) + (ln_w is not None))
        block = S.block()

        @block.sync
        def _(sp):
            if product is not None:
                sp.dma_start(wraw[:], product.rearrange("(k p) n -> p k n", p=P)).then_inc(w_in, 16)
            if gate is not None:
                sp.dma_start(gw[:], gate).then_inc(w_in, 16)
            if ln_w is not None:
                sp.dma_start(lnw[:], ln_w).then_inc(w_in, 16)
            if n_in:
                sp.wait_ge(w_in, n_in)

        @block.tensor
        def _(pe):
            if n_in:
                pe.wait_ge(w_in, n_in)
            if product is not None:
                pe.wait_ge(w_lo, 1)

            def turn(t, u):
                pe.wait_ge(normed, t + 1)
                for k in range(KT):
                    mm = pe.transpose(psX[u][:, k * P:(k + 1) * P], xs[:, u, k * P:(k + 1) * P], G["ident"][:])
                mm.then_inc(turned, 1)

            def use(t, u):
                pe.wait_ge(low, t + 1)
                for k in range(KT):
                    ks = slice(k * P, (k + 1) * P)
                    if logits is not None:
                        mm = pe.matmul(psY[u][:, 0:E], xt[:, u, ks], gw[:, k, :], start=k == 0, stop=k == KT - 1)
                    else:
                        mm = split3(pe, psY[u][:, 0:HID], xh[:, u, ks], xl[:, u, ks], wh[:, k, :], wl[:, k, :],
                                    k == 0, k == KT - 1)
                mm.then_inc(done, 1)

            turn(0, 0)
            with pe.Fori(0, NT // 2 - 1) as i:
                for u in range(2):
                    turn(2 * i + u + 1, 1 - u)
                    use(2 * i + u, u)
            turn(NT - 1, 1)
            use(NT - 2, 0)
            use(NT - 1, 1)

        @block.scalar
        def _(act):
            if n_in:
                act.wait_ge(w_in, n_in)
            if product is not None:
                act.activation(wh[:], wraw[:], ACT.Copy).then_inc(w_hi, 1)
            with act.Fori(0, NT // 2) as i:
                for u in range(2):
                    t = 2 * i + u
                    act.wait_ge(turned, t + 1)
                    for k in range(KT):
                        ks = slice(k * P, (k + 1) * P)
                        sc = lnw[:, k:k + 1] if ln_w is not None else 1.0
                        x = act.activation(xt[:, u, ks], psX[u][:, ks], ACT.Copy, scale=sc)
                    x.then_inc(whole, 1)
                    act.wait_ge(whole, t + 1)
                    act.activation(xh[:, u, :], xt[:, u, :], ACT.Copy).then_inc(high, 1)

        @block.vector
        def _(dve):
            if product is not None:
                dve.wait_ge(w_hi, 1)
                dve.tensor_tensor(wl[:], wraw[:], wh[:].bitcast(F32), ALU.subtract).then_inc(w_lo, 1)

            def norm(t, u):
                x = row(src, t)
                if ln_w is None:
                    dve.tensor_copy(xs[:, u, :], x).then_inc(normed, 1)
                    return
                dve.bn_stats(st[:, 0:6], x)
                dve.drain()
                dve.bn_aggr(mv[:], st[:, 0:6])
                dve.drain()
                dve.scalar_tensor_tensor(mv[:, 1:2], mv[:, 0:1], mv[:, 0:1], mv[:, 1:2], ALU.mult, ALU.add)
                dve.drain()
                dve.tensor_scalar(rin[:, u:u + 1], mv[:, 1:2], EPS, None, ALU.add).then_inc(var, 1)
                dve.wait_ge(rs, t + 1)
                dve.tensor_scalar(xs[:, u, :], x, rstd[:, u:u + 1], None, ALU.mult).then_inc(normed, 1)

            def parts(t, u):
                dve.wait_ge(high, t + 1)
                dve.tensor_tensor(xl[:, u, :], xt[:, u, :], xh[:, u, :].bitcast(F32), ALU.subtract).then_inc(low, 1)
                if keep is not None:
                    for part, kept in ((xh, keep[0]), (xl, keep[1])):
                        if part is xl:
                            dve.drain()
                        dve.tensor_copy(kept[:, :, bass.ds(t * P, P)],
                                        part[:, u, :].bitcast(F32).rearrange("p (k q) -> p k q", k=KT))

            def take(t, u):
                dve.wait_ge(done, t + 1)
                if logits is not None:
                    dve.tensor_copy(row(logits, t), psY[u][:, 0:E]).then_inc(out, 1)
                else:
                    dve.tensor_copy(row(dst, t), psY[u][:, 0:HID]).then_inc(out, 1)

            norm(0, 0)
            parts(0, 0)
            norm(1, 1)
            with dve.Fori(0, NT // 2 - 1) as i:
                for u in range(2):
                    t = 2 * i + u
                    take(t, u)
                    parts(t + 1, 1 - u)
                    dve.drain()
                    norm(t + 2, u)
            take(NT - 2, 0)
            parts(NT - 1, 1)
            take(NT - 1, 1)

        @block.gpsimd
        def _(pool):
            if ln_w is not None:
                with pool.Fori(0, NT // 2) as i:
                    for u in range(2):
                        pool.wait_ge(var, 2 * i + u + 1)
                        pool.tensor_tensor(rstd[:, u:u + 1], rin[:, u:u + 1], G["mhalf"][:, 0:1],
                                           ALU.pow).then_inc(rs, 1)


def route_stage(nc, G, name, logits, softmax_first):
    with Scope(nc, name) as S:
        val = S.sb("val", [P, NT, E])
        best = S.sb("best", [P, NT, 8])
        idx = S.sb("idx", [P, NT, 8], U32)
        fidx = S.sb("fidx", [P, NT, 8])
        g = S.sb("g", [P, 6, NT])
        hot = S.sb("hot", [P, 2, E, NT])
        shifted, powers, first = S.sem("shifted"), S.sem("powers"), S.sem("first")
        block = S.block()

        def wide(ap):
            return ap.rearrange("p (t o) -> p t o", o=1).broadcast_to([P, NT, E])

        @block.scalar
        def _(act):
            act.wait_ge(shifted, 1)
            if softmax_first:
                act.activation(val[:], val[:], ACT.Exp).then_inc(powers, 1)
            else:
                act.activation(g[:, 1, :], g[:, 0, :], ACT.Exp).then_inc(powers, 1)

        @block.vector
        def _(dve):
            if softmax_first:
                dve.tensor_reduce(g[:, 0, :], logits[:], AX.X, ALU.max)
                dve.drain()
                dve.tensor_tensor(val[:], logits[:], wide(g[:, 0, :]), ALU.subtract).then_inc(shifted, 1)
                dve.wait_ge(powers, 1)
                dve.tensor_reduce(g[:, 1, :], val[:], AX.X, ALU.add)
                dve.drain()
                dve.reciprocal(g[:, 2, :], g[:, 1, :])
                dve.drain()
                dve.tensor_tensor(val[:], val[:], wide(g[:, 2, :]), ALU.mult)
            else:
                dve.tensor_copy(val[:], logits[:])
            dve.drain()
            for t in range(NT):
                dve.max(best[:, t, :], val[:, t, :])
            dve.drain()
            for t in range(NT):
                dve.max_index(idx[:, t, :], best[:, t, :], val[:, t, :])
            dve.drain()
            dve.tensor_copy(fidx[:], idx[:])
            if softmax_first:
                dve.tensor_tensor(g[:, 3, :], best[:, :, 0], best[:, :, 1], ALU.add)
                dve.drain()
                dve.reciprocal(g[:, 2, :], g[:, 3, :])
                dve.drain()
                dve.tensor_tensor(g[:, 4, :], best[:, :, 0], g[:, 2, :], ALU.mult)
                dve.tensor_tensor(g[:, 5, :], best[:, :, 1], g[:, 2, :], ALU.mult)
            else:
                dve.tensor_tensor(g[:, 0, :], best[:, :, 1], best[:, :, 0], ALU.subtract).then_inc(shifted, 1)
                dve.wait_ge(powers, 1)
                dve.tensor_scalar(g[:, 2, :], g[:, 1, :], 1.0, None, ALU.add)
                dve.drain()
                dve.reciprocal(g[:, 4, :], g[:, 2, :])
                dve.drain()
                dve.tensor_tensor(g[:, 5, :], g[:, 4, :], g[:, 1, :], ALU.mult)
            dve.drain()
            for k in range(2):
                for e in range(E):
                    dve.scalar_tensor_tensor(hot[:, k, e, :], fidx[:, :, k], float(e), g[:, 4 + k, :],
                                             ALU.is_equal, ALU.mult)
            dve.drain()
            dve.tensor_tensor(G["we"][:], hot[:, 0, :, :], hot[:, 1, :, :], ALU.add)


def experts_stage(nc, G, name, w_in_ap, w_out_ap, ft, xh, xl, acc):
    N = ft * P
    with Scope(nc, name) as S:
        raw = S.sb("raw", [P, 3, KT * N])
        parts = [[S.sb(f"w{u}{q}", [P, 3, KT * N], F32R) for q in "hl"] for u in range(2)]
        sl = S.sb("sl", [P, 2, 512])
        gf = S.sb("gf", [P, 2, 512])
        gh, gl = S.sb("gh", [P, 2, 512], F32R), S.sb("gl", [P, 2, 512], F32R)
        wcur = S.sb("wcur", [P, 2, NT])
        ps1 = [S.ps(f"ps1{i}") for i in range(2)]
        ps3 = [S.ps(f"ps3{i}") for i in range(2)]
        psY = [[S.ps(f"psY{i}{b}") for b in range(2)] for i in range(2)]
        w_in, w_hi, w_lo = S.sem("w_in"), S.sem("w_hi"), S.sem("w_lo")
        hid, act_s, mul_s, g_hi, g_lo = S.sem("hid"), S.sem("silu"), S.sem("mul"), S.sem("g_hi"), S.sem("g_lo")
        y_part, y_done, y_out = S.sem("y_part"), S.sem("y_done"), S.sem("y_out")
        SPE = 2 * ft
        w2v = lambda ap: ap.rearrange("p (f n) -> p f n", n=HID)
        block = S.block()

        def experts(eng, body, lead):
            lead(0, 0)
            with eng.Fori(0, E // 2 - 1) as i:
                body(2 * i, 0, True)
                body(2 * i + 1, 1, True)
            body(E - 2, 0, True)
            body(E - 1, 1, False)

        @block.sync
        def _(sp):
            def load(e, u):
                sp.wait_ge(w_lo, 3 * e)
                for j in range(2):
                    src = w_in_ap[bass.ds(e, 1), :, j, :].rearrange("o (k p) n -> p (o k) n", p=P)
                    sp.dma_start(raw[:, j, :].rearrange("p (k n) -> p k n", k=KT), src).then_inc(w_in, 16)
                sp.dma_start(w2v(raw[:, 2, :]), w_out_ap[bass.ds(e, 1), :, :].rearrange("o (f p) n -> p (o f) n", p=P)).then_inc(w_in, 16)
            load(0, 0)
            with sp.Fori(0, E - 1) as e:
                load(e + 1, 0)

        @block.tensor
        def _(pe):
            def up(e, u, hf, f):
                s = hf * ft + f
                if not (isinstance(e, int) and e == 0 and s < 2):
                    pass
                pe.wait_ge(mul_s, e * SPE + max(0, s - 1)) if s >= 1 else pe.wait_ge(g_hi, e * SPE)
                for j, ps in ((0, ps1), (1, ps3)):
                    for k in range(KT):
                        c = slice(k * N + f * P, k * N + (f + 1) * P)
                        q = slice(hf * 512, hf * 512 + 512)
                        mm = split3(pe, ps[s % 2][:], parts[u][0][:, j, c], parts[u][1][:, j, c], xh[:, k, q], xl[:, k, q],
                                    k == 0, k == KT - 1)
                mm.then_inc(hid, 1)

            def down(e, u, hf, f):
                s = hf * ft + f
                pe.wait_ge(g_lo, e * SPE + s + 1)
                if f == 0:
                    pe.wait_ge(y_out, e * 2 + max(0, hf - 1))
                for q in range(4):
                    out = psY[hf][q // 2][:, (q % 2) * HID:(q % 2 + 1) * HID]
                    c = slice(f * HID, (f + 1) * HID)
                    g = (s % 2, slice(q * P, (q + 1) * P))
                    w2h, w2l = parts[u][0][:, 2, c], parts[u][1][:, 2, c]
                    pe.matmul(out, gh[:, g[0], g[1]], w2h, start=f == 0 and q % 2 == 0, stop=False, skip_group_check=True)
                    pe.matmul(out, gh[:, g[0], g[1]], w2l, start=False, stop=False, skip_group_check=True)
                    mm = pe.matmul(out, gl[:, g[0], g[1]], w2h, start=False, stop=f == ft - 1, skip_group_check=True)
                mm.then_inc(y_part, 1)

            def body(e, u, more):
                pe.wait_ge(w_lo, 3 * (e + 1))
                for s in range(SPE + 1):
                    if s < SPE:
                        up(e, u, s // ft, s % ft)
                    if s >= 1:
                        down(e, u, (s - 1) // ft, (s - 1) % ft)
            experts(pe, body, lambda e, u: None)

        @block.scalar
        def _(act):
            def lead(e, u):
                act.wait_ge(w_in, 48 * (e + 1))
                if not isinstance(e, int) or e >= 2:
                    act.wait_ge(y_part, SPE * (e - 1))
                for j in range(3):
                    act.activation(parts[u][0][:, j, :], raw[:, j, :], ACT.Copy).then_inc(w_hi, 1)

            def body(e, u, more):
                for s in range(SPE):
                    n = e * SPE + s
                    act.wait_ge(hid, n + 1)
                    act.activation(sl[:, s % 2, :], ps1[s % 2][:], ACT.Silu).then_inc(act_s, 1)
                    act.wait_ge(mul_s, n + 1)
                    if s >= 1:
                        act.wait_ge(y_part, n - 1)
                    else:
                        act.wait_ge(y_part, e * SPE)
                    act.activation(gh[:, s % 2, :], gf[:, s % 2, :], ACT.Copy).then_inc(g_hi, 1)
                    if s == SPE - 2 and more:
                        lead(e + 1, 1 - u)
            experts(act, body, lead)

        @block.vector
        def _(dve):
            def lead(e, u):
                for j in range(3):
                    dve.wait_ge(w_hi, 3 * e + j + 1)
                    dve.tensor_tensor(parts[u][1][:, j, :], raw[:, j, :], parts[u][0][:, j, :].bitcast(F32),
                                      ALU.subtract).then_inc(w_lo, 1)
                dve.tensor_copy(wcur[:, u, :], row(G["we"], e))
                dve.drain()

            def take(e, u, hf):
                dve.wait_ge(y_part, e * SPE + (hf + 1) * ft)
                for q in range(4):
                    t = hf * 4 + q
                    i = dve.scalar_tensor_tensor(acc[:, t, :], psY[hf][q // 2][:, (q % 2) * HID:(q % 2 + 1) * HID],
                                                 wcur[:, u, t:t + 1], acc[:, t, :], ALU.mult, ALU.add)
                i.then_inc(y_out, 1)

            def body(e, u, more):
                for s in range(SPE):
                    n = e * SPE + s
                    dve.wait_ge(act_s, n + 1)
                    if s >= 1:
                        dve.wait_ge(g_lo, n - 1)
                    else:
                        dve.wait_ge(g_lo, e * SPE)
                    dve.tensor_tensor(gf[:, s % 2, :], sl[:, s % 2, :], ps3[s % 2][:], ALU.mult).then_inc(mul_s, 1)
                    dve.wait_ge(g_hi, n + 1)
                    dve.tensor_tensor(gl[:, s % 2, :], gf[:, s % 2, :], gh[:, s % 2, :].bitcast(F32),
                                      ALU.subtract).then_inc(g_lo, 1)
                    if s == SPE - 2 and more:
                        lead(e + 1, 1 - u)
                    if s == min(ft + 1, SPE - 1):
                        take(e, u, 0)
                take(e, u, 1)
            experts(dve, body, lead)


def mix_stage(nc, G, name, x, s, y, dst=None, store=None):
    with Scope(nc, name) as S:
        sg = S.sb("sg", [P, NT, HID])
        sig, mul, res, st = S.sem("sig"), S.sem("mul"), S.sem("res"), S.sem("st")
        o = dst if dst is not None else sg
        block = S.block()

        @block.scalar
        def _(act):
            for t in range(0, NT, 2):
                act.activation(sg[:, t:t + 2, :], y[:, t:t + 2, :], ACT.Silu).then_inc(sig, 1)

        @block.vector
        def _(dve):
            for t in range(0, NT, 2):
                dve.wait_ge(sig, t // 2 + 1)
                dve.tensor_tensor(sg[:, t:t + 2, :], sg[:, t:t + 2, :], s[:, t:t + 2, :], ALU.mult).then_inc(mul, 1)
                dve.wait_ge(mul, t // 2 + 1)
                dve.tensor_tensor(o[:, t:t + 2, :], sg[:, t:t + 2, :], x[:, t:t + 2, :], ALU.add).then_inc(res, 1)

        @block.sync
        def _(sp):
            if store is not None:
                for t in range(0, NT, 2):
                    sp.wait_ge(res, t // 2 + 1)
                    sp.dma_start(store.rearrange("(t p) d -> p t d", p=P)[:, t:t + 2, :], o[:, t:t + 2, :]).then_inc(st, 16)
                sp.wait_ge(st, 16 * (NT // 2))


def window_stage(nc, G, name, qkT, vS, o_all):
    with Scope(nc, name) as S:
        k_raw = S.sb("k_raw", [P, T])
        kh, kl = S.sb("kh", [P, T], F32R), S.sb("kl", [P, T], F32R)
        v_raw = S.sb("v_raw", [P, 2, NT, HKV * DV1])
        vh, vl = S.sb("vh", [P, 2, NT, HKV * DV1], F32R), S.sb("vl", [P, 2, NT, HKV * DV1], F32R)
        q_raw = S.sb("q_raw", [P, 2, T])
        qh, ql = S.sb("qh", [P, 2, T], F32R), S.sb("ql", [P, 2, T], F32R)
        pr = S.sb("pr", [P, 3, 256])
        pth, ptl = S.sb("pth", [P, 3, 256], F32R), S.sb("ptl", [P, 3, 256], F32R)
        nm = S.sb("nm", [P, 4])
        rs, rr = S.sb("rs", [P, REP * NT]), S.sb("rr", [P, REP * NT])
        psS = [S.ps(f"psS{i}") for i in range(3)]
        psP = [S.ps(f"psP{i}") for i in range(3)]
        psO = S.ps("psO")
        v_in, v_hi, v_lo = S.sem("v_in"), S.sem("v_hi"), S.sem("v_lo")
        k_in, k_hi, k_lo = S.sem("k_in"), S.sem("k_hi"), S.sem("k_lo")
        q_in, q_hi, q_lo = [S.sem("q_in0"), S.sem("q_in1")], S.sem("q_hi"), S.sem("q_lo")
        scores, negmax, probs = S.sem("scores"), S.sem("negmax"), S.sem("probs")
        turned, pt_hi, pt_lo = S.sem("turned"), S.sem("pt_hi"), S.sem("pt_lo")
        pv, recip, o_out = S.sem("pv"), S.sem("recip"), S.sem("o_out")
        STEPS = REP * NT
        r3 = lambda ap: ap.rearrange("p (t n) -> p t n", t=NT)

        def span(s):
            return slice(P, 256) if s % NT == 0 else slice(0, 256)

        block = S.block()

        @block.sync
        def _(sp):
            sp.dma_start(v_raw[:, 0, :, :], vS).then_inc(v_in, 16)
            sp.dma_start(v_raw[32:P, 1, 1:NT, :], vS[32:P, 0:NT - 1, :]).then_inc(v_in, 16)
            sp.dma_start(v_raw[0:32, 1, 1:NT, :], vS[0:32, 0:1, :].broadcast_to([32, NT - 1, HKV * DV1])).then_inc(v_in, 16)
            with sp.Fori(0, HKV) as g:
                sp.wait_ge(k_lo, g)
                sp.dma_start(r3(k_raw[:]), qkT[:, :, bass.ds(g * D + H * D, D)]).then_inc(k_in, 16)
                for j in range(REP):
                    sp.wait_ge(q_lo, g * REP + max(0, j - 1))
                    sp.dma_start(r3(q_raw[:, j % 2, :]), qkT[:, :, bass.ds(g * (REP * D) + j * D, D)]).then_inc(q_in[j % 2], 16)

        @block.tensor
        def _(pe):
            def score(g, s):
                j, t = divmod(s, NT)
                if t == 0:
                    pe.wait_ge(q_lo, g * REP + j + 1)
                pe.wait_ge(probs, g * STEPS + max(0, s - 2))
                out = psS[s % 3]
                a, b = qh[:, j % 2, t * P:(t + 1) * P], ql[:, j % 2, t * P:(t + 1) * P]
                if t == 0:
                    split3(pe, out[:, P:256], a, b, kh[:, 0:P], kl[:, 0:P], True, False)
                    mask = G["window0"][:]
                    c = slice(P, 256)
                else:
                    split3(pe, out[:, 0:32], a, b, kh[:, 0:32], kl[:, 0:32], True, True)
                    ks = slice(t * P - 96, t * P + P)
                    split3(pe, out[:, 32:256], a, b, kh[:, ks], kl[:, ks], True, False)
                    mask = G["window"][:]
                    c = slice(32, 256)
                pe.matmul(out[:, c], G["identb"][:], mask, start=False, stop=True).then_inc(scores, 1)

            def turn(g, s):
                pe.wait_ge(probs, g * STEPS + s + 1)
                pe.wait_ge(pt_lo, g * STEPS + max(0, s - 2))
                for b in range(0 if s % NT else 1, 2):
                    mm = pe.transpose(psP[s % 3][:, b * P:(b + 1) * P], pr[:, s % 3, b * P:(b + 1) * P], G["ident"][:])
                mm.then_inc(turned, 1)

            def values(g, s):
                t = s % NT
                pe.wait_ge(pt_lo, g * STEPS + s + 1)
                out = psO[:, s * DV1:(s + 1) * DV1]
                for b in range(1 if t == 0 else 0, 2):
                    c = slice(b * P, (b + 1) * P)
                    mm = split3(pe, out, pth[:, s % 3, c], ptl[:, s % 3, c], vg(vh, 1 - b, t), vg(vl, 1 - b, t),
                                b == (1 if t == 0 else 0), b == 1)
                mm.then_inc(pv, 1)

            with pe.Fori(0, HKV) as g:
                pe.wait_ge(k_lo, g + 1)
                pe.wait_ge(v_lo, g + 1)

                def vg(v, b, t):
                    return v[:, b, t, 0:DV1]
                for s in range(STEPS + 4):
                    if s < STEPS:
                        score(g, s)
                    if 2 <= s < STEPS + 2:
                        turn(g, s - 2)
                    if s == 4:
                        pe.wait_ge(o_out, g)
                    if s >= 4:
                        values(g, s - 4)

        @block.scalar
        def _(act):
            def q_part(g, j):
                act.wait_ge(q_in[j % 2], 16 * (g * (REP // 2) + j // 2 + 1))
                act.wait_ge(scores, g * STEPS + max(0, (j - 1) * NT))
                act.activation(qh[:, j % 2, :], q_raw[:, j % 2, :], ACT.Copy).then_inc(q_hi, 1)

            act.wait_ge(v_in, 48)
            with act.Fori(0, HKV) as g:
                act.wait_ge(pv, g * STEPS)
                act.wait_ge(k_in, g * 16 + 16)
                act.activation(kh[:], k_raw[:], ACT.Copy).then_inc(k_hi, 1)
                for s in range(STEPS + 3):
                    if s < STEPS and s == 0:
                        q_part(g, 0)
                    if s < STEPS and s % NT == NT - 3 and s // NT + 1 < REP:
                        q_part(g, s // NT + 1)
                    if s >= 3:
                        n = s - 3
                        act.wait_ge(turned, g * STEPS + n + 1)
                        act.wait_ge(pv, g * STEPS + max(0, n - 2))
                        act.activation(pth[:, n % 3, span(n)], psP[n % 3][:, span(n)], ACT.Copy).then_inc(pt_hi, 1)
                    if s < STEPS:
                        act.wait_ge(negmax, g * STEPS + s + 1)
                        act.wait_ge(turned, g * STEPS + max(0, s - 2))
                        if s == 0:
                            act.wait_ge(recip, g)
                        act.activation(pr[:, s % 3, span(s)], psS[s % 3][:, span(s)], ACT.Exp,
                                       bias=nm[:, s % 4:s % 4 + 1], accum_out=rs[:, s:s + 1]).then_inc(probs, 1)

        @block.vector
        def _(dve):
            def q_part(g, j):
                dve.wait_ge(q_hi, g * REP + j + 1)
                dve.tensor_tensor(ql[:, j % 2, :], q_raw[:, j % 2, :], qh[:, j % 2, :].bitcast(F32),
                                  ALU.subtract).then_inc(q_lo, 1)

            dve.wait_ge(v_in, 48)
            with dve.Fori(0, HKV) as g:
                dve.wait_ge(k_hi, g + 1)
                dve.tensor_tensor(kl[:], k_raw[:], kh[:].bitcast(F32), ALU.subtract).then_inc(k_lo, 1)
                for b, ts in ((0, slice(0, NT)), (1, slice(1, NT))):
                    src_v = v_raw[:, b, ts, bass.ds(g * DV1, DV1)]
                    dve.tensor_copy(vh[:, b, ts, 0:DV1], src_v)
                    dve.drain()
                    i = dve.tensor_tensor(vl[:, b, ts, 0:DV1], src_v, vh[:, b, ts, 0:DV1].bitcast(F32), ALU.subtract)
                i.then_inc(v_lo, 1)
                for s in range(STEPS + 3):
                    if s < STEPS and s == 0:
                        q_part(g, 0)
                    if s < STEPS and s % NT == NT - 3 and s // NT + 1 < REP:
                        q_part(g, s // NT + 1)
                    if s < STEPS:
                        dve.wait_ge(scores, g * STEPS + s + 1)
                        dve.tensor_reduce(nm[:, s % 4:s % 4 + 1], psS[s % 3][:, span(s)], AX.X, ALU.max,
                                          negate=True).then_inc(negmax, 1)
                    if s >= 3:
                        n = s - 3
                        dve.wait_ge(pt_hi, g * STEPS + n + 1)
                        dve.tensor_tensor(ptl[:, n % 3, span(n)], psP[n % 3][:, span(n)],
                                          pth[:, n % 3, span(n)].bitcast(F32), ALU.subtract).then_inc(pt_lo, 1)
                dve.reciprocal(rr[:], rs[:]).then_inc(recip, 1)
                dve.wait_ge(pv, g * STEPS + STEPS)
                dve.wait_ge(recip, g + 1)
                for j in range(REP):
                    n = slice(j * NT, (j + 1) * NT)
                    i = dve.tensor_tensor(o_all[:, :, bass.ds(g * (REP * DV1) + j * DV1, DV1)],
                                          psO[:, j * NT * DV1:(j + 1) * NT * DV1].rearrange("p (t d) -> p t d", t=NT),
                                          rr[:, n].rearrange("p (t o) -> p t o", o=1).broadcast_to([P, NT, DV1]), ALU.mult)
                i.then_inc(o_out, 1)


def fold_stage(nc, G, name, w_up, w_down, lora, gate_w, gate_lora, up_eff, down_eff, gate_eff):
    NL = HID + 2 * I1 + I1 + HID
    with Scope(nc, name) as S:
        lr = S.sb("lr", [R1, 2, NL])
        wr = S.sb("wr", [P, 2, 3, HID])
        we = S.sb("we", [P, 2, 3, HID])
        gl = S.sb("gl", [R1, HID + E])
        gw = S.sb("gw", [P, KT, E])
        ps = [[S.ps(f"ps{u}{b}") for b in range(2)] for u in range(2)]
        psg = S.ps("psg")
        g_in, g_mm, g_out = S.sem("g_in"), S.sem("g_mm"), S.sem("g_out")
        w_in = [S.sem("w_in0"), S.sem("w_in1")]
        w_st = [S.sem("w_st0"), S.sem("w_st1")]
        mm_s, add_s = S.sem("mm"), S.sem("add")
        block = S.block()

        @block.sync
        def _(sp):
            sp.dma_start(gl[:], gate_lora).then_inc(g_in, 16)
            sp.dma_start(gw[:], gate_w).then_inc(g_in, 16)
            with sp.Fori(0, E // 2) as i:
                for u in range(2):
                    e = 2 * i + u
                    sp.wait_ge(add_s, 2 * i)
                    sp.dma_start(lr[:, u, :], lora[bass.ds(e, 1), :, :].rearrange("o r n -> r (o n)")).then_inc(w_in[u], 16)
                    sp.dma_start(wr[:, u, 0:KT, :], w_up[bass.ds(e, 1), :, :].rearrange("o (k p) n -> p (o k) n", p=P)).then_inc(w_in[u], 16)
                    sp.dma_start(wr[:, u, KT, :], w_down[bass.ds(e, 1), :, :].rearrange("o p n -> p (o n)")).then_inc(w_in[u], 16)

        @block.tensor
        def _(pe):
            pe.wait_ge(g_in, 32)
            for k in range(KT):
                mm = pe.matmul(psg[:, k * E:(k + 1) * E], gl[:, k * P:(k + 1) * P], gl[:, HID:HID + E], start=True, stop=True)
            mm.then_inc(g_mm, 1)
            with pe.Fori(0, E // 2) as i:
                for u in range(2):
                    pe.wait_ge(w_in[u], i * 48 + 48)
                    pe.wait_ge(add_s, 2 * i)
                    for k in range(KT):
                        pe.matmul(ps[u][0][:, k * HID:(k + 1) * HID], lr[:, u, k * P:(k + 1) * P],
                                  lr[:, u, HID:2 * HID], start=True, stop=True)
                    pe.matmul(ps[u][1][:, 0:HID], lr[:, u, 2 * HID:2 * HID + I1], lr[:, u, 2 * HID + I1:NL],
                              start=True, stop=True).then_inc(mm_s, 1)

        @block.vector
        def _(dve):
            dve.wait_ge(g_mm, 1)
            dve.scalar_tensor_tensor(gate_eff[:], psg[:, 0:KT * E].rearrange("p (k e) -> p k e", k=KT), 2.0, gw[:],
                                     ALU.mult, ALU.add)
            with dve.Fori(0, E // 2) as i:
                for u in range(2):
                    dve.wait_ge(mm_s, 2 * i + u + 1)
                    dve.wait_ge(w_st[u], i * 32)
                    dve.scalar_tensor_tensor(we[:, u, 0:KT, :], ps[u][0][:].rearrange("p (k n) -> p k n", k=KT), 2.0,
                                             wr[:, u, 0:KT, :], ALU.mult, ALU.add)
                    dve.scalar_tensor_tensor(we[:, u, KT, :], ps[u][1][:, 0:HID], 2.0, wr[:, u, KT, :], ALU.mult,
                                             ALU.add).then_inc(add_s, 1)

        @block.scalar
        def _(act):
            with act.Fori(0, E // 2) as i:
                for u in range(2):
                    e = 2 * i + u
                    act.wait_ge(add_s, e + 1)
                    act.dma_start(up_eff[bass.ds(e, 1), :, :, :].rearrange("o (k p) j n -> p (o k) (j n)", p=P),
                                  we[:, u, 0:KT, :]).then_inc(w_st[u], 16)
                    act.dma_start(down_eff[bass.ds(e, 1), :, :].rearrange("o p n -> p (o n)"), we[:, u, KT, :]).then_inc(w_st[u], 16)
            for u in range(2):
                act.wait_ge(w_st[u], 32 * (E // 2))


def build(nc, a, out):
    def dram(n, s):
        return nc.dram_tensor(n, s, F32, **({"kind": "ExternalOutput"} if DEBUG else {})).ap()

    def show(n, ap):
        if not DEBUG:
            return
        d = nc.dram_tensor("d_" + n, list(ap.shape), F32, kind="ExternalOutput").ap()
        with Scope(nc, "show_" + n) as S:
            st = S.sem("st")
            block = S.block()

            @block.sync
            def _(sp):
                sp.dma_start(d, ap[:]).then_inc(st, 16)
                sp.wait_ge(st, 16)

    qkT_a, vS_a, oT_a, rS_a = dram("qkT_a", [P, NT, QK]), dram("vS_a", [P, NT, 512]), dram("oT_a", [P, NT, H * D]), dram("rS_a", [P, P])
    qkT_b, vS_b, oT_b, rS_b = dram("qkT_b", [P, NT, QK]), dram("vS_b", [P, NT, 512]), dram("oT_b", [P, NT, H * D]), dram("rS_b", [P, P])
    qkT_c, vS_c = dram("qkT_c", [P, NT, QK]), dram("vS_c", [P, NT, HKV * DV1])
    up_eff, down_eff = dram("up_eff", [E, HID, 2, I1]), dram("down_eff", [E, I1, HID])
    with Scope(nc, "g") as S:
        G = {k: S.sb(k, [P, NT, HID]) for k in ("x", "xn", "s", "x2")}
        G["ident"] = S.sb("ident", [P, P])
        G["identb"] = S.sb("identb", [P, P], BF16)
        G["causal"] = S.sb("causal", [P, P], BF16)
        G["window0"] = S.sb("window0", [P, P], BF16)
        G["window"] = S.sb("window", [P, 224], BF16)
        G["mhalf"] = S.sb("mhalf", [P, 32])
        G["we"] = S.sb("we", [P, E, NT])
        gate_eff = S.sb("gate_eff", [P, KT, E])
        logits = S.sb("logits", [P, NT, E])
        load_stage(nc, G, a)
        fold_stage(nc, G, "fo", a["w_up1"], a["w_down1"], a["lora1"], a["gate_w1"], a["gate_lora1"], up_eff, down_eff, gate_eff)
        if DEBUG != "l1":
            prep_stage(nc, G, "pa", G["x"], a["w_qkv_a"], a["rope_a"], qkT_a, vS_a, 512,
                       gains=(a["qn_g"], a["kn_g"], a["qn_b"], a["kn_b"]), keep_xn=G["xn"])
            attention_stage(nc, G, "aa", qkT_a, vS_a, oT_a, rS_a)
            prep_stage(nc, G, "pb", G["xn"], a["w_qkv_b"], a["rope_b"], qkT_b, vS_b, 512, rms=True, ln_w=a["ln_w"])
            attention_stage(nc, G, "ab", qkT_b, vS_b, oT_b, rS_b)
            heads_out_stage(nc, G, "ho", ((oT_a, rS_a, a["w_o_a"]), (oT_b, rS_b, a["w_o_b"])))
            show("s_all", G["s"])
            show("x2_all", G["x2"])
            with Scope(nc, "m0") as M:
                xh, xl = M.sb("xh", [P, KT, T], F32R), M.sb("xl", [P, KT, T], F32R)
                rows_stage(nc, G, "r0", G["x2"], ln_w=a["ff_ln_w"], keep=(xh, xl), gate=a["gate_w0"], logits=logits)
                route_stage(nc, G, "g0", logits, False)
                show("we0", G["we"])
                experts_stage(nc, G, "e0", a["w_up0"], a["w_down0"], FT, xh, xl, G["x2"])
            mix_stage(nc, G, "x0", G["x"], G["s"], G["x2"], dst=G["x"])
        show("x1_all", G["x"])
        prep_stage(nc, G, "pc", G["x"], a["w_qkv_c"], a["rope_c"], qkT_c, vS_c, HKV * DV1, keep_xn=G["xn"])
        window_stage(nc, G, "wa", qkT_c, vS_c, G["x2"])
        rows_stage(nc, G, "ro", G["x2"], product=a["w_o_c"], dst=G["s"])
        show("s1", G["s"])
        with Scope(nc, "m1") as M:
            xh, xl = M.sb("xh", [P, KT, T], F32R), M.sb("xl", [P, KT, T], F32R)
            rows_stage(nc, G, "r1", G["xn"], keep=(xh, xl), gate_sb=gate_eff, logits=logits)
            route_stage(nc, G, "g1", logits, True)
            zero_stage(nc, G["x2"])
            experts_stage(nc, G, "e1", up_eff, down_eff, 1, xh, xl, G["x2"])
        show("y1", G["x2"])
        mix_stage(nc, G, "x1", G["x"], G["s"], G["x2"], store=out)


def zero_stage(nc, ap):
    with Scope(nc, "z") as S:
        block = S.block()

        @block.vector
        def _(dve):
            dve.memset(ap[:], 0.0)



def rope_tables(inv, scale_q):
    ang = np.outer(np.arange(T, dtype=np.float32), inv).astype(np.float32)
    cos, sin = np.cos(ang.astype(np.float64)), np.sin(ang.astype(np.float64))
    c, s = np.concatenate([cos, cos], 1), np.concatenate([-sin, sin], 1)
    both = [c, s] if scale_q is None else [c * scale_q, s * scale_q, c, s]
    return np.ascontiguousarray(np.stack(both, 1).astype(np.float32))


def kernel(**inputs):
    import ml_dtypes
    import concourse.bacc as bacc
    from concourse.bass_utils import run_bass_kernel_spmd

    a = {k: np.asarray(v) for k, v in inputs.items()}
    bf = ml_dtypes.bfloat16
    turn = (np.arange(NQK)[:, None] * D + np.concatenate([np.arange(0, D, 2), np.arange(1, D, 2)])).ravel()
    tq, tk = turn[:H * D], turn[:HKV * D]
    sc = float(D) ** -0.5
    step = np.arange(0, D, 2)
    inv_a = np.float32(1) / (1e6 ** (step / D)).astype(np.float32)
    inv_b = (1e6 ** (-step / D)).astype(np.float32)
    inv_c = (1.0 / np.float32(1e4) ** (step.astype(np.float32) / np.float32(D))).astype(np.float32)
    i, j = np.arange(P)[:, None], np.arange(P)[None, :]
    seen = ((j <= i) & (j > i - 64)) | ((j < 32) & (j <= i - 64))
    j = np.arange(-96, P)[None, :]
    band = (j <= i) & (j > i - 64)
    laid = {
        "x": a["L0_attn_x"].reshape(T, HID),
        "ident": np.eye(P, dtype=np.float32),
        "identb": np.eye(P, dtype=np.float32).astype(bf),
        "causal": np.where(np.tril(np.ones((P, P))) > 0, 0.0, NEG).astype(bf),
        "w_qkv_a": a["L0_attn_w_qkv"].T,
        "rope_a": rope_tables(inv_a, None),
        "qn_g": a["L0_attn_qn_g"], "qn_b": a["L0_attn_qn_b"], "kn_g": a["L0_attn_kn_g"], "kn_b": a["L0_attn_kn_b"],
        "w_qkv_b": np.concatenate([a["L0_ffn_wq"][:, tq], a["L0_ffn_wk"][:, tk], a["L0_ffn_wv"]], 1),
        "rope_b": rope_tables(inv_b, sc),
        "w_o_a": a["L0_attn_w_o"].T, "w_o_b": a["L0_ffn_wo"],
        "ff_ln_w": a["L0_ffn_ff_ln_w"].reshape(KT, P).T,
        "gate_w0": a["L0_ffn_gate_w"].reshape(KT, P, E).transpose(1, 0, 2),
        "w_up0": np.stack([a["L0_ffn_w1"], a["L0_ffn_w3"]], 2), "w_down0": a["L0_ffn_w2"],
        "w_qkv_c": np.concatenate([a["L1_attn_wq"][:, tq], a["L1_attn_wk"][:, tk], a["L1_attn_wv"]], 1),
        "rope_c": rope_tables(inv_c, sc),
        "window0": np.where(seen[:, :P], 0.0, NEG).astype(bf), "window": np.where(band, 0.0, NEG).astype(bf),
        "w_o_c": a["L1_attn_wo"],
        "w_up1": a["L1_ffn_gate_up_proj"], "w_down1": a["L1_ffn_down_proj"],
        "lora1": np.concatenate([a["L1_ffn_gup_lora_A"], a["L1_ffn_gup_lora_B"].transpose(0, 2, 1),
                                 a["L1_ffn_down_lora_A"], a["L1_ffn_down_lora_B"].transpose(0, 2, 1)], 2),
        "gate_w1": a["L1_ffn_gate_weight"].T.reshape(KT, P, E).transpose(1, 0, 2),
        "gate_lora1": np.concatenate([a["L1_ffn_gate_lora_A"], a["L1_ffn_gate_lora_B"].T], 1),
        "ln_w": a["L0_ffn_ln_w"].reshape(KT, P).T,
    }
    nc = bacc.Bacc("TRN2", target_bir_lowering=False, num_devices=1)
    arrays, args = {}, {}
    for name, v in laid.items():
        v = np.ascontiguousarray(v)
        arrays[f"in_{name}"] = v
        args[name] = nc.dram_tensor(f"in_{name}", v.shape, mybir.dt.from_np(v.dtype), kind="ExternalInput").ap()
    out = nc.dram_tensor("out", (1, T, HID), F32, kind="ExternalOutput").ap()
    build(nc, args, out.rearrange("o t d -> (o t) d"))
    r = run_bass_kernel_spmd(nc, [arrays], core_ids=[0])
    return r.results[0]["out"]
```
